# Optimizing a Trainium2 kernel written in Bass

```python
import numpy as np
import jax
import jax.numpy as jnp

def _softmax(x, axis=-1):
    return jax.nn.softmax(x, axis=axis)
def _gelu(x):
    return jax.nn.gelu(x, approximate=True)
def _silu(x):
    return jax.nn.silu(x)
def _sigmoid(x):
    return jax.nn.sigmoid(x)
def _layernorm(x, axis=-1, eps=1e-5):
    m = jnp.mean(x, axis=axis, keepdims=True)
    v = jnp.var(x, axis=axis, keepdims=True)
    return (x - m) / jnp.sqrt(v + eps)
def _scatter_add(tgt, idx, src, axis=0):
    return tgt.at[idx].add(src)
def _segment_sum(src, seg, n):
    return jax.ops.segment_sum(src, seg, n)

kernel_name = 'mk_metaformer_d1_conv_nchw384_898b98'

def setup_inputs(seed: int = 0):
    np.random.seed(seed)
    _w = jnp.asarray
    def _rec_inputs():
        import jax
        import jax.numpy as jnp
        _gk = jax.random.key(seed)
        x = -0.0001538 + 1 * jax.random.normal(jax.random.fold_in(_gk, 1), (4, 384, 64, 64), jnp.float32)
        return x
    x = _rec_inputs()
    def _L0_conv_setup():
        import jax, jax.numpy as jnp
        import numpy as np
        DIM = 384
        PD = 96
        QK = 16
        VD = PD
        QKV_OUT = 2 * QK + VD
        EPS = 1e-05

        def _bn(y, g, b, m, v):
            inv = g / jnp.sqrt(v + EPS)
            return y * inv[None, :, None, None] + (b - m * inv)[None, :, None, None]
        key = jax.random.key(seed)
        ks = jax.random.split(key, 12)
        B, H, W = (4, 64, 64)
        x = jax.random.normal(ks[0], (B, DIM, H, W), dtype=jnp.float32)
        ln_w = jnp.ones((PD,), jnp.float32)
        ln_b = jnp.zeros((PD,), jnp.float32)
        w_qkv = jax.random.normal(ks[1], (QKV_OUT, PD), jnp.float32) * 0.05
        bn1_g = jax.random.uniform(ks[2], (QKV_OUT,), jnp.float32, 0.5, 1.5)
        bn1_b = jax.random.normal(ks[3], (QKV_OUT,), jnp.float32) * 0.05
        bn1_m = jax.random.normal(ks[4], (QKV_OUT,), jnp.float32) * 0.05
        bn1_v = jax.random.uniform(ks[5], (QKV_OUT,), jnp.float32, 0.5, 1.5)
        w_proj = jax.random.normal(ks[6], (DIM, DIM), jnp.float32) * 0.02
        bn2_g = jax.random.uniform(ks[7], (DIM,), jnp.float32, 0.5, 1.5)
        bn2_b = jax.random.normal(ks[8], (DIM,), jnp.float32) * 0.05
        bn2_m = jax.random.normal(ks[9], (DIM,), jnp.float32) * 0.05
        bn2_v = jax.random.uniform(ks[10], (DIM,), jnp.float32, 0.5, 1.5)
        return {'x': x, 'ln_w': ln_w, 'ln_b': ln_b, 'w_qkv': w_qkv, 'bn1_g': bn1_g, 'bn1_b': bn1_b, 'bn1_m': bn1_m, 'bn1_v': bn1_v, 'w_proj': w_proj, 'bn2_g': bn2_g, 'bn2_b': bn2_b, 'bn2_m': bn2_m, 'bn2_v': bn2_v}
    _L0_conv_all = _L0_conv_setup()
    _L0_conv_in = {k: v for k, v in _L0_conv_all.items() if k in ('ln_w', 'ln_b', 'w_qkv', 'bn1_g', 'bn1_b', 'bn1_m', 'bn1_v', 'w_proj', 'bn2_g', 'bn2_b', 'bn2_m', 'bn2_v', )}
    del _L0_conv_all

    def _L0_ffn_setup():
        import jax, jax.numpy as jnp
        import numpy as np
        D_MODEL = 384
        D_FF = 1536
        key = jax.random.key(seed)
        k_x, k1, k2, k3, k4 = jax.random.split(key, 5)
        std = 0.02
        return {'x': jax.random.normal(k_x, (16, 2048, D_MODEL), dtype=jnp.float32), 'c_fc_1': std * jax.random.normal(k1, (1536, 32), dtype=jnp.float32), 'c_fc_2': std * jax.random.normal(k2, (1, 12), dtype=jnp.float32), 'c_proj_1': std * jax.random.normal(k3, (32, 1536), dtype=jnp.float32), 'c_proj_2': std * jax.random.normal(k4, (12, 1), dtype=jnp.float32)}
    _L0_ffn_all = _L0_ffn_setup()
    _L0_ffn_in = {k: v for k, v in _L0_ffn_all.items() if k in ('c_fc_1', 'c_fc_2', 'c_proj_1', 'c_proj_2', )}
    del _L0_ffn_all

    return {
        "x": x,
        "L0_conv_ln_w": _L0_conv_in["ln_w"],
        "L0_conv_ln_b": _L0_conv_in["ln_b"],
        "L0_conv_w_qkv": _L0_conv_in["w_qkv"],
        "L0_conv_bn1_g": _L0_conv_in["bn1_g"],
        "L0_conv_bn1_b": _L0_conv_in["bn1_b"],
        "L0_conv_bn1_m": _L0_conv_in["bn1_m"],
        "L0_conv_bn1_v": _L0_conv_in["bn1_v"],
        "L0_conv_w_proj": _L0_conv_in["w_proj"],
        "L0_conv_bn2_g": _L0_conv_in["bn2_g"],
        "L0_conv_bn2_b": _L0_conv_in["bn2_b"],
        "L0_conv_bn2_m": _L0_conv_in["bn2_m"],
        "L0_conv_bn2_v": _L0_conv_in["bn2_v"],
        "L0_ffn_c_fc_1": _L0_ffn_in["c_fc_1"],
        "L0_ffn_c_fc_2": _L0_ffn_in["c_fc_2"],
        "L0_ffn_c_proj_1": _L0_ffn_in["c_proj_1"],
        "L0_ffn_c_proj_2": _L0_ffn_in["c_proj_2"],
    }

def reference(x, L0_conv_ln_w, L0_conv_ln_b, L0_conv_w_qkv, L0_conv_bn1_g, L0_conv_bn1_b, L0_conv_bn1_m, L0_conv_bn1_v, L0_conv_w_proj, L0_conv_bn2_g, L0_conv_bn2_b, L0_conv_bn2_m, L0_conv_bn2_v, L0_ffn_c_fc_1, L0_ffn_c_fc_2, L0_ffn_c_proj_1, L0_ffn_c_proj_2):
    import jax
    import jax.numpy as jnp
    def _L0_conv_ref(x, ln_w, ln_b, w_qkv, bn1_g, bn1_b, bn1_m, bn1_v, w_proj, bn2_g, bn2_b, bn2_m, bn2_v):
        import jax, jax.numpy as jnp
        import numpy as np
        DIM = 384
        PD = 96
        QK = 16
        VD = PD
        QKV_OUT = 2 * QK + VD
        EPS = 1e-05

        def _bn(y, g, b, m, v):
            inv = g / jnp.sqrt(v + EPS)
            return y * inv[None, :, None, None] + (b - m * inv)[None, :, None, None]
        B, C, H, W = x.shape
        N = H * W
        scale = QK ** (-0.5)
        x_attn = x[:, :PD]
        x_skip = x[:, PD:]
        u = x_attn.mean(axis=1, keepdims=True)
        s = ((x_attn - u) ** 2).mean(axis=1, keepdims=True)
        xn = (x_attn - u) / jnp.sqrt(s + EPS)
        xn = xn * ln_w[None, :, None, None] + ln_b[None, :, None, None]
        qkv = jnp.einsum('oc,bchw->bohw', w_qkv, xn)
        qkv = _bn(qkv, bn1_g, bn1_b, bn1_m, bn1_v)
        q = qkv[:, :QK].reshape(B, QK, N)
        k = qkv[:, QK:2 * QK].reshape(B, QK, N)
        v = qkv[:, 2 * QK:].reshape(B, VD, N)
        attn = jax.nn.softmax(jnp.einsum('bcn,bcm->bnm', q, k) * scale, axis=-1)
        out = jnp.einsum('bcn,bmn->bcm', v, attn).reshape(B, VD, H, W)
        xm = jax.nn.relu(jnp.concatenate([out, x_skip], axis=1))
        y = jnp.einsum('oc,bchw->bohw', w_proj, xm)
        y = _bn(y, bn2_g, bn2_b, bn2_m, bn2_v)
        return y

    def _L0_ffn_ref(x, c_fc_1, c_fc_2, c_proj_1, c_proj_2):
        import jax, jax.numpy as jnp
        import numpy as np
        D_MODEL = 384
        D_FF = 1536
        w_fc = jnp.kron(c_fc_1, c_fc_2)
        w_proj = jnp.kron(c_proj_1, c_proj_2)
        h = x @ w_fc.T
        h = jax.nn.gelu(h, approximate=False)
        out = h @ w_proj.T
        return out

    def _gn(v, G=32, eps=1e-5):
        B_, C_, H_, W_ = v.shape
        g = v.reshape(B_, G, C_ // G, H_, W_)
        m = jnp.mean(g, axis=(2, 3, 4), keepdims=True)
        s = jnp.var(g, axis=(2, 3, 4), keepdims=True)
        return ((g - m) / jnp.sqrt(s + eps)).reshape(v.shape)

    def _ln_c(v, eps=1e-6):
        m = jnp.mean(v, axis=1, keepdims=True)
        s = jnp.var(v, axis=1, keepdims=True)
        return (v - m) / jnp.sqrt(s + eps)

    def _ln_t(v, eps=1e-5):
        m = jnp.mean(v, axis=-1, keepdims=True)
        s = jnp.var(v, axis=-1, keepdims=True)
        return (v - m) / jnp.sqrt(s + eps)

    def _to_tokens(v):
        B_, C_, H_, W_ = v.shape
        return v.reshape(B_, C_, H_ * W_).transpose(0, 2, 1)
    def _from_tokens(t, like):
        B_, C_, H_, W_ = like.shape
        return t.transpose(0, 2, 1).reshape(B_, C_, H_, W_)

    x = x + _L0_conv_ref(_ln_c(x), L0_conv_ln_w, L0_conv_ln_b, L0_conv_w_qkv, L0_conv_bn1_g, L0_conv_bn1_b, L0_conv_bn1_m, L0_conv_bn1_v, L0_conv_w_proj, L0_conv_bn2_g, L0_conv_bn2_b, L0_conv_bn2_m, L0_conv_bn2_v)
    t = _to_tokens(x)
    t = t + _L0_ffn_ref(_ln_t(t), L0_ffn_c_fc_1, L0_ffn_c_fc_2, L0_ffn_c_proj_1, L0_ffn_c_proj_2)
    x = _from_tokens(t, x)
    return x


_drawn_inputs = setup_inputs


def setup_inputs(seed=0):
    import zlib

    import numpy as np

    out = dict(_drawn_inputs(seed))
    spreads = {'L0_conv_ln_w': (1.0, 0.6), 'L0_conv_ln_b': (0.0, 0.8)}
    factors = {'L0_conv_w_qkv': 8.0,
     'L0_conv_bn1_g': 8.0,
     'L0_conv_bn1_b': 8.0,
     'L0_conv_bn1_m': 8.0,
     'L0_conv_bn1_v': 8.0,
     'L0_ffn_c_fc_1': 8.0,
     'L0_ffn_c_fc_2': 8.0,
     'L0_ffn_c_proj_1': 8.0,
     'L0_ffn_c_proj_2': 8.0,
     'L0_conv_bn2_b': 4.595,
     'L0_conv_bn2_m': 4.16}
    for name, (base, spread) in spreads.items():
        noise = np.random.default_rng([zlib.crc32(name.encode()), seed]).standard_normal(out[name].shape)
        drawn = base * np.exp(spread * noise) if base else spread * noise
        out[name] = jnp.asarray(drawn.astype(out[name].dtype))
    for name, factor in factors.items():
        out[name] = (out[name] * factor).astype(out[name].dtype)
    return out
```

```python
from contextlib import ExitStack

import numpy as np
import concourse.bass as bass
from concourse import mybir

F32, F16, BF16 = mybir.dt.float32, mybir.dt.float16, mybir.dt.bfloat16
ALU = mybir.AluOpType
ACT = mybir.ActivationFunctionType
AX = mybir.AxisListType
ds = bass.ds

B, C, H, W = 4, 384, 64, 64
N = H * W
P = 128
PD, QK = 96, 16
QKV = 2 * QK + PD
KT = C // P
CH = 512
NCH = N // CH
TPC = CH // P
NT = N // P
DFF, DR, DB = 1536, 32, 12
JT = DFF // P
SK = C - PD
NSTK = 6 * QK
NROW = NSTK + 3
VP = 2 * PD + 2
VN = 2 * PD + 1
KPU = 2
NU = NT // KPU
UW = KPU * CH
RING = 4

LN_IN_EPS, LN_ATTN_EPS, LN_FFN_EPS, BN_EPS = 1e-6, 1e-5, 1e-5, 1e-5
F16_TOP = 2.0 ** 14
SKIP_SCALE = 2.0 ** 9
U_SCALE = 2.0 ** 9
W_TOP = 2.0 ** 12
TINY = 1e-30
LOG_TOP = float(np.log(F16_TOP))
SCALE = QK ** -0.5

POOL_LOW = (0, 1, 3, 4, 6, 7, 9, 10, 12)
DVE_HIGH = (13, 15)
DVE_LOW = tuple(i for i in range(NU) if i not in POOL_LOW)
ACT_HIGH = tuple(i for i in range(NU) if i not in DVE_HIGH)
MAX_AT = [3, 2, 3, 2, 3, 2, 3, 2, 3, 2, 3, 2, 2, 0, 0, 0]
MAX_ROWS_AT = 13
NMX = TPC * NCH
N_LOADS = 20
MXC = NMX + 2


def build(nc, A):
    ctx = ExitStack()
    with ctx:
        def sb(name, shape, dt=F32):
            return ctx.enter_context(nc.sbuf_tensor(name, shape, dt))

        def sem(name):
            return ctx.enter_context(nc.semaphore(name))

        ident = sb("ident", [P, P])
        ident_h = sb("ident_h", [P, P], F16)
        ident_b = sb("ident_b", [P, P], BF16)
        ones = sb("ones", [P, P])
        expo = sb("expo", [P, 8])
        half = sb("half", [P, 1])
        log_top = sb("log_top", [P, 1])
        w_qkv = sb("w_qkv", [PD, QKV])
        bias_qkv = sb("bias_qkv", [P, QKV])
        wp_hi = sb("wp_hi", [P, KT, C], F16)
        wp_lo = sb("wp_lo", [P, KT, C], F16)
        wp_unscale = sb("wp_unscale", [P, KT])
        shift2 = sb("shift2", [P, KT])
        fold = sb("fold", [P, KT, DR])
        fc1 = sb("fc1", [3 * DR, DFF], F16)
        gelu_scale = sb("gelu_scale", [P, JT])
        p1t = sb("p1t", [P, JT, DR])
        spread = sb("spread", [P, C])
        ks = sb("ks", [P, N], BF16)
        qs = sb("qs", [P, N], BF16)
        vs = sb("vs", [P, NT, VP], F16)
        xm_hi = sb("xm_hi", [P, NT, C], F16)
        xm_lo = sb("xm_lo", [P, NT, C], F16)
        xin = sb("xin", [P, 2, KT, CH])
        pool32 = sb("pool32", [P, 8192])
        p32 = pool32[:, 0:RING * UW].rearrange("p (r n) -> p r n", r=RING)
        p_hi = pool32[:, 4096:6144].bitcast(F16).rearrange("p (r n) -> p r n", r=RING)
        p_lo = pool32[:, 6144:8192].bitcast(F16).rearrange("p (r n) -> p r n", r=RING)
        gel = pool32[:, 0:JT * CH].rearrange("p (j n) -> p j n", j=JT)
        skipf = pool32[:, 0:2 * TPC * SK].rearrange("p (s t n) -> p s t n", s=2, t=TPC)
        qkvf = sb("qkvf", [P, 2, TPC, QKV])
        rest = sb("rest", [P, 2, TPC, 2 * QK])
        parts = sb("parts", [P, 2, TPC, 3, 2 * QK], BF16)
        stk = sb("stk", [P, 2, TPC, 2 * P], BF16)
        bst = sb("bst", [P, 2, TPC, 2, 6])
        mv = sb("mv", [P, 2, TPC, 2, 2])
        var = sb("var", [P, 2, 2, TPC])
        rstd = sb("rstd", [P, 2, 2, TPC])
        skip_s = sb("skip_s", [P, 2, TPC])
        skip_b = sb("skip_b", [P, 2, TPC])
        mxp = sb("mxp", [P, TPC, NCH])
        nm = sb("nm", [P, TPC])
        nmr = sb("nmr", [P, TPC])
        nms = sb("nms", [P, TPC, 3], BF16)
        acs = sb("acs", [P, TPC, VP])
        attn = sb("attn", [P, TPC, PD])
        rsum = sb("rsum", [P, TPC])
        xc = sb("xc", [P, KT, 2, CH], F16)
        yb = sb("yb", [P, KT, CH])
        x1 = sb("x1", [P, 2, KT, CH])
        cst = sb("cst", [P, 2, TPC, 6])
        cmv = sb("cmv", [P, 2, TPC, 2])
        cvar = sb("cvar", [P, 2, TPC])
        crstd = sb("crstd", [P, 2, TPC])
        uraw = sb("uraw", [P, 2, TPC, DR])
        uf = sb("uf", [P, 2, TPC, DR])
        us = sb("us", [P, 2, TPC, 3 * DR], F16)
        uc = sb("uc", [3 * DR, CH], F16)
        zs = sb("zs", [P, CH])
        outb = sb("outb", [P, 2, KT, CH])
        raw_qkv = sb("raw_qkv", [P, PD])
        lnw = sb("lnw", [P, PD])
        lnb = sb("lnb", [P, PD])
        bn1 = sb("bn1", [P, 4])
        bn2 = sb("bn2", [P, 4, KT])
        bvar = sb("bvar", [P, 4])
        binv = sb("binv", [P, 4])
        sc = sb("sc", [P, 16])
        diag = sb("diag", [P, P])
        fccol = sb("fccol", [DB, 4])
        rep = sb("rep", [DB, C])
        p2b = sb("p2b", [DB, P])
        blk = sb("blk", [P, KT, DR])
        blkt = sb("blkt", [P, C])
        fmax = sb("fmax", [P, JT])
        fsig = sb("fsig", [P, JT])
        wmax = sb("wmax", [P, KT])
        raw_p = pool32[:, 0:1152].rearrange("p (t n) -> p t n", t=KT)
        wph0 = pool32[:, 1152:1728].bitcast(F16).rearrange("p (t n) -> p t n", t=KT)
        wpl0 = pool32[:, 1728:2304].bitcast(F16).rearrange("p (t n) -> p t n", t=KT)
        colscale = pool32[:, 2304:2688]
        raw_f = pool32[:, 2688:3072].rearrange("p (j n) -> p j n", j=JT)
        fstk = pool32[:, 3072:3648].bitcast(F16).rearrange("p (j n) -> p j n", j=JT)
        raw_p1 = pool32[0:DR, 3648:5184]
        w1 = pool32[:, 5184:5280]
        junk = pool32[:, 5280:5376]

        ps = ctx.enter_context(nc.psum_tensor("ps", [P, 8, 512], F32))

        def bank16(b, dt):
            return ps[:, b, :].bitcast(dt)

        w_loaded = sem("w_loaded")
        set_dve = sem("set_dve")
        set_pe = sem("set_pe")
        set_pool = sem("set_pool")
        bn_var_ready = sem("bn_var_ready")
        norm_ready = sem("norm_ready")
        w1_ready = sem("w1_ready")
        tau_ready = sem("tau_ready")
        wp_ready = sem("wp_ready")
        set_up = sem("set_up")
        x_loaded = [sem("x_loaded0"), sem("x_loaded1")]
        x_free = sem("x_free")
        tok_ready = sem("tok_ready")
        a_banks_free = sem("a_banks_free")
        a_stat = sem("a_stat")
        a_var = sem("a_var")
        a_rstd = sem("a_rstd")
        a_skip = sem("a_skip")
        a_parts = sem("a_parts")
        a_qkv = sem("a_qkv")
        stk_ready = sem("stk_ready")
        stk_turned = sem("stk_turned")
        skip_f = sem("skip_f")
        skip_hi = sem("skip_hi")
        skip_lo = sem("skip_lo")
        v_hi = sem("v_hi")
        v_lo = sem("v_lo")
        st_ready = sem("st_ready")
        exp_done = sem("exp_done")
        high_act = sem("high_act")
        high_dve = sem("high_dve")
        low_dve = sem("low_dve")
        low_pool = sem("low_pool")
        pv_done = sem("pv_done")
        mx_ready = sem("mx_ready")
        mx_free = sem("mx_free")
        nm_step = sem("nm_step")
        acs_ready = sem("acs_ready")
        passed = sem("passed")
        post = sem("post")
        xt_ready = sem("xt_ready")
        xt_copied = sem("xt_copied")
        y_ready = sem("y_ready")
        y_scaled = sem("y_scaled")
        x1_ready = sem("x1_ready")
        u_ready = sem("u_ready")
        u_taken = sem("u_taken")
        c_stat = sem("c_stat")
        c_var = sem("c_var")
        c_rstd = sem("c_rstd")
        u_split = sem("u_split")
        ut_ready = sem("ut_ready")
        ut_copied = sem("ut_copied")
        h_ready = sem("h_ready")
        g_ready = sem("g_ready")
        z_ready = sem("z_ready")
        z_copied = sem("z_copied")
        ff_ready = sem("ff_ready")
        out_ready = sem("out_ready")
        stored = [sem("stored0"), sem("stored1")]

        x_v = A["x"].rearrange("b (k p) h w -> p b k (h w)", p=P)
        out_v = A["out"].rearrange("b (k p) h w -> p b k (h w)", p=P)

        block = ctx.enter_context(nc.Block())

        @block.sync
        def _(sp):
            def col(v):
                return v.rearrange("(p o) -> p o", o=1)

            loads = [
                (ident[:, :], A["ident"]), (rep[:, :], A["rep"]),
                (blk[:, :, :], A["blk"].rearrange("(k p) a -> p k a", p=P)), (blkt[:, :], A["blkt"]),
                (raw_qkv[:, :], A["w_qkv"]),
                (lnw[:, :], A["ln_w"].partition_broadcast(P)), (lnb[:, :], A["ln_b"].partition_broadcast(P)),
                (bn1[:, 0:1], col(A["bn1_g"])), (bn1[:, 1:2], col(A["bn1_b"])),
                (bn1[:, 2:3], col(A["bn1_m"])), (bn1[:, 3:4], col(A["bn1_v"])),
                (bn2[:, 0, :], A["bn2_g"].rearrange("(k p) -> p k", p=P)),
                (bn2[:, 1, :], A["bn2_b"].rearrange("(k p) -> p k", p=P)),
                (bn2[:, 2, :], A["bn2_m"].rearrange("(k p) -> p k", p=P)),
                (bn2[:, 3, :], A["bn2_v"].rearrange("(k p) -> p k", p=P)),
                (raw_p, A["w_proj"].rearrange("(k p) c -> p k c", p=P)),
                (raw_f, A["c_fc_1"].rearrange("(j p) a -> p j a", p=P)),
                (raw_p1, A["c_proj_1"]),
                (fccol[:, 0:1], A["c_fc_2"].rearrange("a b -> b a")), (fccol[:, 1:2], A["c_proj_2"]),
            ]
            assert len(loads) == N_LOADS
            with nc.allow_non_contiguous_dma(reason="small vectors, once"):
                for dst, src in loads:
                    sp.dma_start(dst, src).then_inc(w_loaded, 16)

            def load_x(b, j, s, n):
                sp.wait_ge(x_free, n + 1)
                src = x_v[:, ds(b, 1), :, ds(j * CH, CH)].rearrange("p o k n -> p (o k) n")
                sp.dma_start(xin[:, s, :, :], src).then_inc(x_loaded[s], 16)

            def store(b, j, s, q):
                sp.wait_ge(out_ready, (q + 1) * KT)
                dst = out_v[:, ds(b, 1), :, ds(j * CH, CH)].rearrange("p o k n -> p (o k) n")
                sp.dma_start(dst, outb[:, s, :, :]).then_inc(stored[s], 16)

            with sp.Fori(0, B) as b:
                with sp.Fori(0, NCH // 2) as jj:
                    for s in range(2):
                        load_x(b, jj * 2 + s, s, b * (2 * NCH) + jj * 2 + s)
                for s in range(2):
                    load_x(b, s, s, b * (2 * NCH) + NCH + s)
                with sp.Fori(0, NCH // 2 - 1) as jj:
                    for s in range(2):
                        store(b, jj * 2 + s, s, b * NCH + jj * 2 + s)
                        load_x(b, jj * 2 + (s + 2), s, b * (2 * NCH) + jj * 2 + (NCH + s + 2))
                for j in (NCH - 2, NCH - 1):
                    store(b, j, j % 2, b * NCH + j)
            for s in range(2):
                sp.wait_ge(stored[s], 16 * B * NCH // 2)

        @block.tensor
        def _(pe):
            mm = pe.matmul

            pe.wait_ge(w1_ready, 1)
            pe.transpose(ps[0:PD, 0, 0:P], w1, ident[:, :])
            mm(ps[:, 1, 0:P], ones[:, :], diag[:, :], start=True, stop=True).then_inc(set_pe, 1)
            pe.wait_ge(tau_ready, 1)
            mm(ps[:, 2, 0:PD], ones[:, :], diag[:, 2 * QK:], start=True, stop=True).then_inc(set_pe, 1)
            mm(ps[:, 3, 0:1], ones[0:DB, :], fccol[:, 0:1], start=True, stop=True)
            mm(ps[:, 3, 1:2], ones[0:DB, :], fccol[:, 2:3], start=True, stop=True)
            for k in range(KT):
                mm(ps[:, 3, 2 + k:3 + k], rep[:, k * P:(k + 1) * P], fccol[:, 0:1], start=True, stop=True)
            mm(ps[:, 4, 0:C], p2b[:, :], rep[:, :], start=True, stop=True).then_inc(set_pe, 1)
            for j in range(JT):
                last = pe.transpose(ps[:, 5, j * DR:(j + 1) * DR], raw_p1[:, j * P:(j + 1) * P], ident[0:DR, 0:DR])
            last.then_inc(set_pe, 1)
            pe.wait_ge(wp_ready, 1)
            for k in range(KT):
                for part, src in ((0, wph0), (1, wpl0)):
                    for o in range(KT):
                        last = pe.transpose(bank16((6, 7, 0)[k], F16)[:, part * 512 + o * P:part * 512 + (o + 1) * P],
                                            src[:, o, k * P:(k + 1) * P], ident_h[:, :])
            for j in range(JT):
                last = pe.transpose(bank16(1 + j // 8, F16)[0:3 * DR, (j % 8) * P:(j % 8 + 1) * P],
                                    fstk[:, j, :], ident_h[:, :])
            last.then_inc(set_pe, 1)
            pe.wait_ge(set_up, 1)

            def tokens(b, jj, s):
                q = b * NCH + jj * 2 + s
                pe.wait_ge(x_loaded[s], (b * NCH + jj + 1) * 16)
                pe.wait_ge(a_banks_free, q + 1)
                for t in range(TPC):
                    bk = 4 * s + t
                    for k in range(KT):
                        pe.transpose(ps[:, bk, k * P:(k + 1) * P], xin[:, s, k, t * P:(t + 1) * P], ident[:, :])
                    mm(ps[:, bk, C:C + QKV], xin[0:PD, s, 0, t * P:(t + 1) * P], w_qkv[:, :],
                       start=True, stop=True).then_inc(tok_ready, 1)

            def turn_stacks(q, s):
                pe.wait_ge(stk_ready, q + 1)
                pe.wait_ge(skip_f, q + 1)
                for t in range(TPC):
                    bk = bank16(4 * s + t, BF16)
                    pe.transpose(bk[0:NROW, 2 * C:2 * C + P], stk[:, s, t, 0:NROW], ident_b[:, :])
                    last = pe.transpose(bk[0:NSTK, 2 * C + P:2 * C + 2 * P], stk[:, s, t, P:P + NSTK], ident_b[:, :])
                last.then_inc(stk_turned, 1)

            def max_tile(gq, g, idx):
                t, c = divmod(idx, NCH)
                pe.wait_ge(mx_free, gq * MXC + idx + 1)
                mm(ps[:, 4 + idx % 2, :], qs[0:NSTK, ds(g * CH + t * P, P)], ks[0:NSTK, c * CH:(c + 1) * CH],
                   start=True, stop=True).then_inc(mx_ready, 1)

            def max_rows(gq):
                pe.wait_ge(mx_free, gq * MXC + NMX + 1)
                pe.wait_ge(nm_step, (gq + 1) * 5)
                for t in range(TPC):
                    last = pe.transpose(bank16(4, BF16)[0:3, t * P:(t + 1) * P], nms[:, t, :], ident_b[:, :])
                last.then_inc(mx_ready, 1)

            def scores(gq, g, i):
                n = gq * NU + i
                if i == 0:
                    pe.wait_ge(mx_free, (gq + 1) * MXC + 2)
                pe.wait_ge(exp_done, n + 1)
                for h in range(KPU):
                    kt = KPU * i + h
                    last = mm(ps[:, 2 * (i % 2) + h, :], ks[0:NROW, kt * P:(kt + 1) * P], qs[0:NROW, ds(g * CH, CH)],
                              start=True, stop=True)
                last.then_inc(st_ready, 1)

            def values(gq, i):
                if i in POOL_LOW:
                    pe.wait_ge(low_pool, (gq + 1) * len(POOL_LOW) + (POOL_LOW.index(i) + 1))
                else:
                    pe.wait_ge(low_dve, (gq + 1) * len(DVE_LOW) + (DVE_LOW.index(i) + 1))
                if i == 0:
                    pe.wait_ge(acs_ready, gq * 2 + 0)
                for h in range(KPU):
                    kt = KPU * i + h
                    for t in range(TPC):
                        acc = ps[:, 6 + t // 2, (t % 2) * VP:(t % 2) * VP + VN]
                        at = h * CH + t * P
                        mm(acc, p_hi[:, i % RING, at:at + P], vs[:, kt, 0:VN],
                           start=(kt == 0 and t % 2 == 0), stop=False, skip_group_check=True)
                        last = mm(acc[:, 0:PD + 1], p_lo[:, i % RING, at:at + P], vs[:, kt, 0:PD + 1],
                                  start=False, stop=(kt == NT - 1), skip_group_check=True)
                last.then_inc(pv_done, 1)

            def group(gq, g, last_group):
                idx = 0
                for i in range(NU):
                    if not last_group:
                        for _ in range(MAX_AT[i]):
                            max_tile(gq + 1, g + 1, idx)
                            idx += 1
                    if i + 2 < NU:
                        scores(gq, g, i + 2)
                    elif not last_group:
                        scores(gq + 1, g + 1, i + 2 - NU)
                    values(gq, i)
                    if i == MAX_ROWS_AT and not last_group:
                        max_rows(gq + 1)

            def turn_input(b, j, q):
                for k in range(KT):
                    bk = bank16(2 + k % 2, F16)
                    if k == 2:
                        pe.wait_ge(xt_copied, q * KT + 1)
                    for part, src in ((0, xm_hi), (1, xm_lo)):
                        for t in range(TPC):
                            last = pe.transpose(bk[:, part * CH + t * P:part * CH + (t + 1) * P],
                                                src[:, ds(j * TPC + t, 1), k * P:(k + 1) * P].rearrange("p o n -> p (o n)"),
                                                ident_h[:, :])
                    last.then_inc(xt_ready, 1)

            def project(q):
                pe.wait_ge(xt_copied, (q + 1) * KT)
                for o in range(KT):
                    bk = ps[:, 4 + o % 2, :]
                    if o < 2:
                        pe.wait_ge(out_ready, q * KT)
                    else:
                        pe.wait_ge(y_scaled, q * KT + 1)
                    n = 0
                    for k in range(KT):
                        for w, part in ((wp_hi, 0), (wp_lo, 0), (wp_hi, 1)):
                            last = mm(bk, w[:, k, o * P:(o + 1) * P], xc[:, k, part, :], start=(n == 0), stop=(n == 8))
                            n += 1
                    last.then_inc(y_ready, 1)

            def fold_u(q, s):
                pe.wait_ge(x1_ready, (q + 1) * KT)
                for t in range(TPC):
                    pe.wait_ge(u_taken, q * TPC + t + 1)
                    bk = ps[:, t % 2, :]
                    for k in range(KT):
                        pe.transpose(bk[:, k * P:(k + 1) * P], x1[:, s, k, t * P:(t + 1) * P], ident[:, :])
                    for k in range(KT):
                        last = mm(bk[:, C:C + DR], x1[:, s, k, t * P:(t + 1) * P], fold[:, k, :],
                                  start=(k == 0), stop=(k == KT - 1), skip_group_check=True)
                    last.then_inc(u_ready, 1)

            def ffn(q, s):
                pe.wait_ge(u_split, (q + 1) * 4)
                for t in range(TPC):
                    last = pe.transpose(bank16(3, F16)[0:3 * DR, t * P:(t + 1) * P], us[:, s, t, :], ident_h[:, :])
                last.then_inc(ut_ready, 1)
                pe.wait_ge(ut_copied, q + 1)

                def up(j):
                    pe.wait_ge(g_ready, q * JT + j + 1)
                    mm(ps[:, 6 + j % 2, :], fc1[:, j * P:(j + 1) * P], uc[:, :], start=True, stop=True).then_inc(h_ready, 1)

                def down(r):
                    pe.wait_ge(g_ready, q * JT + 4 * r + 4 + 2)
                    for c in range(4):
                        last = mm(ps[c * DR:(c + 1) * DR, 2, :], p1t[:, 4 * r + c, :], gel[:, 4 * r + c, :],
                                  start=(r == 0), stop=(r == JT // 4 - 1), tile_position=(0, c * DR))
                    if r == JT // 4 - 1:
                        last.then_inc(z_ready, 1)

                for j in range(JT):
                    up(j)
                    if j == 5:
                        down(0)
                    if j == 9:
                        down(1)
                down(2)

            def expand(q):
                pe.wait_ge(z_copied, q + 1)
                for o in range(KT):
                    if o == 2:
                        pe.wait_ge(out_ready, q * KT + 1)
                    mm(ps[:, 4 + o % 2, :], spread[:, o * P:(o + 1) * P], zs[:, :], start=True, stop=True).then_inc(ff_ready, 1)

            with pe.Fori(0, B) as b:
                pe.wait_ge(out_ready, b * (NCH * KT))
                pe.sem_inc(passed, 1)
                with pe.Fori(0, NCH // 2) as jj:
                    for s in range(2):
                        tokens(b, jj, s)
                        turn_stacks(b * NCH + jj * 2 + s, s)
                gq0 = b * NCH
                pe.wait_ge(a_banks_free, gq0 + NCH + 2)
                pe.wait_ge(v_lo, gq0 + NCH)
                for idx in range(NMX):
                    max_tile(gq0, 0, idx)
                max_rows(gq0)
                scores(gq0, 0, 0)
                scores(gq0, 0, 1)
                with pe.Fori(0, NCH - 1) as g:
                    group(b * NCH + g, g, False)
                group(gq0 + (NCH - 1), NCH - 1, True)

                pe.wait_ge(post, (gq0 + NCH) * 5)
                pe.wait_ge(skip_lo, gq0 + NCH)
                pe.sem_inc(passed, 1)
                with pe.Fori(0, NCH // 2) as jj:
                    for s in range(2):
                        q = b * NCH + jj * 2 + s
                        turn_input(b, jj * 2 + s, q)
                        project(q)
                        fold_u(q, s)
                        ffn(q, s)
                        expand(q)

        @block.scalar
        def _(act):
            act.sem_inc(exp_done, 2)
            act.sem_inc(a_banks_free, 2)
            act.sem_inc(g_ready, 2)

            def skip_values(b, jj, s):
                q = b * NCH + jj * 2 + s
                act.wait_ge(tok_ready, q * TPC + TPC)
                act.wait_ge(a_qkv, q * 4 + 1)
                act.wait_ge(skip_lo, q)
                for t in range(TPC):
                    last = act.activation(skipf[:, s, t, :], ps[:, 4 * s + t, PD:C], ACT.Relu,
                                          bias=skip_b[:, s, t:t + 1], scale=skip_s[:, s, t:t + 1])
                last.then_inc(skip_f, 1)
                act.wait_ge(skip_f, q + 1)
                act.activation(xm_hi[:, ds((jj * 2 + s) * TPC, TPC), PD:C], skipf[:, s, :, :],
                               ACT.Copy).then_inc(skip_hi, 1)

            def stacks(b, jj, s):
                q = b * NCH + jj * 2 + s
                act.wait_ge(stk_turned, q + 1)
                src = ps[:, 4 * s:4 * s + 4, :].bitcast(BF16)
                at = ds((jj * 2 + s) * CH, CH)
                act.activation(ks[0:NROW, at].rearrange("p (t n) -> p t n", t=TPC),
                               src[0:NROW, :, 2 * C:2 * C + P], ACT.Copy)
                act.activation(qs[0:NSTK, at].rearrange("p (t n) -> p t n", t=TPC),
                               src[0:NSTK, :, 2 * C + P:2 * C + 2 * P], ACT.Copy).then_inc(a_banks_free, 1)

            def exponentials(gq, i):
                n = gq * NU + i
                j = (i - RING) % NU
                if j in POOL_LOW:
                    act.wait_ge(low_pool, (gq + (1 if i >= RING else 0)) * len(POOL_LOW) + (POOL_LOW.index(j) + 1))
                else:
                    act.wait_ge(low_dve, (gq + (1 if i >= RING else 0)) * len(DVE_LOW) + (DVE_LOW.index(j) + 1))
                act.wait_ge(st_ready, n + 1)
                act.activation(p32[:, i % RING, :].rearrange("p (h n) -> p h n", h=KPU),
                               ps[:, 2 * (i % 2):2 * (i % 2) + 2, :], ACT.Exp,
                               bias=log_top[:, 0:1], scale=SCALE).then_inc(exp_done, 1)

            def high(gq, i):
                if i not in ACT_HIGH:
                    return
                n = gq * NU + i
                act.wait_ge(exp_done, n + 3)
                act.wait_ge(pv_done, n + 1)
                act.activation(p_hi[:, i % RING, :], p32[:, i % RING, :], ACT.Copy).then_inc(high_act, 1)

            def take_accumulators(gq):
                act.wait_ge(pv_done, (gq + 1) * NU + RING)
                act.wait_ge(post, gq * 5)
                for h in range(2):
                    act.activation(acs[:, 2 * h:2 * h + 2, 0:VN],
                                   ps[:, 6 + h, 0:2 * VP].rearrange("p (t n) -> p t n", t=2)[:, :, 0:VN],
                                   ACT.Copy).then_inc(acs_ready, 1)

            def group(gq, first, last_group):
                for i in range(NU):
                    if i + 1 < NU:
                        exponentials(gq, i + 1)
                    elif not last_group:
                        exponentials(gq + 1, 0)
                    high(gq, i)
                    if i == 0 and not first:
                        take_accumulators(gq - 1)

            def project_out(q, s):
                for o in range(KT):
                    act.wait_ge(y_ready, q * KT + o + 1)
                    act.wait_ge(x1_ready, q * KT)
                    act.activation(yb[:, o, :], ps[:, 4 + o % 2, :], ACT.Identity,
                                   bias=shift2[:, o:o + 1], scale=wp_unscale[:, o:o + 1]).then_inc(y_scaled, 1)

            def gelus(q):
                act.wait_ge(z_ready, q)
                for j in range(JT):
                    act.wait_ge(h_ready, q * JT + j + 1)
                    act.activation(gel[:, j, :], ps[:, 6 + j % 2, :], ACT.Gelu,
                                   scale=gelu_scale[:, j:j + 1]).then_inc(g_ready, 1)

            act.wait_ge(set_up, 1)
            with act.Fori(0, B) as b:
                with act.Fori(0, NCH // 2) as jj:
                    for s in range(2):
                        skip_values(b, jj, s)
                        stacks(b, jj, s)
                gq0 = b * NCH
                act.wait_ge(skip_lo, gq0 + NCH)
                exponentials(gq0, 0)
                group(gq0, True, False)
                with act.Fori(1, NCH - 1) as g:
                    group(b * NCH + g, False, False)
                group(gq0 + (NCH - 1), False, True)
                take_accumulators(gq0 + (NCH - 1))
                with act.Fori(0, NCH // 2) as jj:
                    for s in range(2):
                        q = b * NCH + jj * 2 + s
                        project_out(q, s)
                        gelus(q)

        @block.vector
        def _(v):
            v.sem_inc(x_free, 2)
            v.sem_inc(mx_free, 2)
            v.sem_inc(low_dve, len(DVE_LOW))
            v.sem_inc(pv_done, RING)
            v.sem_inc(u_taken, 2)
            steps = [0]

            def link(ins):
                steps[0] += 1
                ins.then_inc(set_dve, 1)
                v.wait_ge(set_dve, steps[0])

            link(v.memset(ones[:, :], 1.0))
            link(v.memset(expo[:, :], -0.5))
            link(v.memset(half[:, :], 0.5))
            link(v.memset(log_top[:, :], LOG_TOP))
            link(v.memset(stk[:, :, :, :], 1.0))
            link(v.memset(vs[:, :, :], 1.0))
            v.wait_ge(w_loaded, 16 * N_LOADS)
            link(v.tensor_copy(ident_h[:, :], ident[:, :]))
            link(v.tensor_copy(ident_b[:, :], ident[:, :]))
            link(v.tensor_scalar(bvar[:, 0:1], bn1[:, 3:4], BN_EPS, None, ALU.add))
            link(v.tensor_scalar(bvar[:, 1:4], bn2[:, 3, :], BN_EPS, None, ALU.add))
            v.sem_inc(bn_var_ready, 1)
            v.wait_ge(set_pool, 1)
            link(v.tensor_tensor(binv[:, 0:1], binv[:, 0:1], bn1[:, 0:1], ALU.mult))
            link(v.tensor_tensor(binv[:, 1:4], binv[:, 1:4], bn2[:, 0, :], ALU.mult))
            link(v.tensor_tensor(junk, raw_qkv[:, :], lnb[:, :], ALU.mult))
            link(v.tensor_reduce(sc[:, 0:1], junk, AX.X, ALU.add))
            link(v.tensor_tensor(sc[:, 0:1], sc[:, 0:1], bn1[:, 2:3], ALU.subtract))
            link(v.scalar_tensor_tensor(sc[:, 0:1], sc[:, 0:1], binv[:, 0:1], bn1[:, 1:2], ALU.mult, ALU.add))
            link(v.scalar_tensor_tensor(w1, raw_qkv[:, :], binv[:, 0:1], lnw[:, :], ALU.mult, ALU.mult))
            link(v.tensor_reduce(sc[:, 1:2], w1, AX.X, ALU.add))
            link(v.tensor_scalar(sc[:, 1:2], sc[:, 1:2], 1.0 / PD, None, ALU.mult))
            link(v.tensor_scalar(w1, w1, sc[:, 1:2], None, ALU.subtract))
            link(v.tensor_tensor(junk, w1, w1, ALU.mult))
            link(v.tensor_reduce(sc[:, 2:3], junk, AX.X, ALU.add))
            link(v.tensor_scalar(sc[:, 2:3], sc[:, 2:3], float(PD), None, ALU.mult))
            v.sem_inc(norm_ready, 1)
            v.wait_ge(set_pool, 2)
            link(v.tensor_reduce(sc[:, 3:4], sc[:, 0:1], AX.X, ALU.max, apply_absolute_value=True))
            link(v.tensor_tensor(sc[:, 3:4], sc[:, 3:4], sc[:, 4:5], ALU.add))
            link(v.tensor_scalar(sc[:, 3:4], sc[:, 3:4], TINY, 1.0 / F16_TOP, ALU.max, ALU.mult))
            link(v.memset(sc[0:2 * QK, 3:4], 1.0))
            link(v.reciprocal(sc[:, 5:6], sc[:, 3:4]))
            link(v.tensor_scalar(w1, w1, sc[:, 5:6], None, ALU.mult))
            link(v.tensor_tensor(sc[:, 6:7], sc[:, 0:1], sc[:, 5:6], ALU.mult))
            link(v.tensor_scalar(diag[:, :], ident[:, :], sc[:, 6:7], None, ALU.mult))
            v.sem_inc(w1_ready, 1)
            v.wait_ge(set_pe, 1)
            link(v.tensor_copy(w_qkv[:, :], ps[0:PD, 0, 0:P]))
            link(v.tensor_copy(bias_qkv[:, :], ps[:, 1, 0:P]))
            link(v.tensor_scalar(p2b[:, :], ones[0:DB, :], fccol[:, 1:2], None, ALU.mult))
            link(v.tensor_reduce(fccol[:, 2:3], fccol[:, 0:1], AX.X, ALU.max, apply_absolute_value=True))
            link(v.tensor_scalar(diag[:, :], ident[:, :], sc[:, 3:4], None, ALU.mult))
            v.sem_inc(tau_ready, 1)
            v.wait_ge(set_pe, 2)
            link(v.tensor_copy(colscale[:, 0:PD], ps[:, 2, 0:PD]))
            link(v.memset(colscale[:, PD:C], 1.0 / SKIP_SCALE))
            for o in range(KT):
                link(v.scalar_tensor_tensor(raw_p[:, o, :], raw_p[:, o, :], binv[:, 1 + o:2 + o], colscale,
                                            ALU.mult, ALU.mult))
            link(v.tensor_reduce(wmax[:, :], raw_p, AX.X, ALU.max, apply_absolute_value=True))
            link(v.tensor_scalar(wp_unscale[:, :], wmax[:, :], TINY, 1.0 / W_TOP, ALU.max, ALU.mult))
            link(v.reciprocal(wmax[:, :], wp_unscale[:, :]))
            for o in range(KT):
                link(v.tensor_scalar(raw_p[:, o, :], raw_p[:, o, :], wmax[:, o:o + 1], None, ALU.mult))
            link(v.tensor_copy(wph0, raw_p))
            link(v.tensor_tensor(wpl0, raw_p, wph0, ALU.subtract))
            link(v.tensor_tensor(shift2[:, :], bn2[:, 2, :], binv[:, 1:4], ALU.mult))
            link(v.tensor_tensor(shift2[:, :], bn2[:, 1, :], shift2[:, :], ALU.subtract))
            link(v.tensor_reduce(fmax[:, :], raw_f, AX.X, ALU.max, apply_absolute_value=True))
            link(v.tensor_scalar(fmax[:, :], fmax[:, :], TINY, 1.0 / F16_TOP, ALU.max, ALU.mult))
            link(v.reciprocal(fsig[:, :], fmax[:, :]))
            link(v.tensor_tensor(raw_f, raw_f, fsig[:, :].unsqueeze(2).to_broadcast([P, JT, DR]), ALU.mult))
            link(v.tensor_copy(fstk[:, :, 0:DR], raw_f))
            link(v.tensor_copy(fstk[:, :, 2 * DR:3 * DR], raw_f))
            link(v.tensor_tensor(fstk[:, :, DR:2 * DR], raw_f, fstk[:, :, 0:DR], ALU.subtract))
            v.sem_inc(wp_ready, 1)
            v.wait_ge(set_pe, 3)
            link(v.tensor_scalar(sc[:, 7:8], ps[:, 3, 0:1], 1.0 / C, None, ALU.mult))
            link(v.tensor_scalar(sc[:, 8:9], ps[:, 3, 1:2], TINY, 1.0 / U_SCALE, ALU.max, ALU.mult))
            link(v.tensor_copy(sc[:, 10:13], ps[:, 3, 2:5]))
            link(v.reciprocal(sc[:, 9:10], sc[:, 8:9]))
            for k in range(KT):
                link(v.tensor_scalar(fold[:, k, :], blk[:, k, :], sc[:, 10 + k:11 + k], sc[:, 7:8],
                                     ALU.mult, ALU.subtract))
            link(v.tensor_scalar(fold[:, :, :], fold[:, :, :], sc[:, 9:10], None, ALU.mult))
            link(v.tensor_scalar(gelu_scale[:, :], fmax[:, :], sc[:, 8:9], None, ALU.mult))
            link(v.tensor_tensor(spread[:, :], ps[:, 4, 0:C], blkt[:, :], ALU.mult))
            v.wait_ge(set_pe, 4)
            link(v.tensor_copy(p1t[:, :, :], ps[:, 5, 0:JT * DR].rearrange("p (j a) -> p j a", j=JT)))
            v.wait_ge(set_pe, 5)
            for k in range(KT):
                src = bank16((6, 7, 0)[k], F16)
                link(v.tensor_copy(wp_hi[:, k, :], src[:, 0:C]))
                link(v.tensor_copy(wp_lo[:, k, :], src[:, 512:512 + C]))
            link(v.tensor_copy(fc1[:, 0:1024], bank16(1, F16)[0:3 * DR, :]))
            link(v.tensor_copy(fc1[:, 1024:DFF], bank16(2, F16)[0:3 * DR, 0:512]))
            v.sem_inc(set_up, 1)

            def statistics(q, s):
                for t in range(TPC):
                    v.wait_ge(tok_ready, q * TPC + t + 1)
                    v.bn_stats(bst[:, s, t, 0, :], ps[:, 4 * s + t, 0:C])
                    v.bn_stats(bst[:, s, t, 1, :], ps[:, 4 * s + t, 0:PD]).then_inc(a_stat, 1)
                v.wait_ge(a_stat, q * (TPC + 2) + TPC)
                v.sem_inc(passed, 1)
                for t in range(TPC):
                    v.bn_aggr(mv[:, s, t, 0, :], bst[:, s, t, 0, :])
                    last = v.bn_aggr(mv[:, s, t, 1, :], bst[:, s, t, 1, :])
                last.then_inc(a_stat, 1)
                v.wait_ge(a_stat, q * (TPC + 2) + TPC + 1)
                v.tensor_scalar(var[:, s, 0, :], mv[:, s, :, 0, 1], LN_IN_EPS, None, ALU.add).then_inc(a_stat, 1)
                v.wait_ge(a_stat, q * (TPC + 2) + TPC + 2)
                v.scalar_tensor_tensor(var[:, s, 1, :], var[:, s, 0, :], LN_ATTN_EPS, mv[:, s, :, 1, 1],
                                       ALU.mult, ALU.add).then_inc(a_var, 1)

            def qkv_parts(b, jj, s):
                q = b * NCH + jj * 2 + s
                v.wait_ge(a_rstd, q + 1)
                v.tensor_scalar(skip_s[:, s, :], rstd[:, s, 0, :], SKIP_SCALE, None, ALU.mult).then_inc(a_skip, 1)
                v.wait_ge(a_skip, q * 2 + 1)
                v.scalar_tensor_tensor(skip_b[:, s, :], mv[:, s, :, 0, 0], -1.0, skip_s[:, s, :],
                                       ALU.mult, ALU.mult).then_inc(a_skip, 1)
                v.wait_ge(v_lo, q)
                for t in range(TPC):
                    last = v.scalar_tensor_tensor(qkvf[:, s, t, :], ps[:, 4 * s + t, C:C + QKV], rstd[:, s, 1, t:t + 1],
                                                  bias_qkv[:, :], ALU.mult, ALU.add)
                last.then_inc(a_qkv, 1)
                v.wait_ge(a_qkv, q * 4 + 1)
                v.tensor_copy(parts[:, s, :, 0, :], qkvf[:, s, :, 0:2 * QK]).then_inc(a_qkv, 1)
                v.tensor_copy(vs[:, ds((jj * 2 + s) * TPC, TPC), 0:PD], qkvf[:, s, :, 2 * QK:]).then_inc(v_hi, 1)
                v.wait_ge(a_qkv, q * 4 + 2)
                v.tensor_tensor(rest[:, s, :, :], qkvf[:, s, :, 0:2 * QK], parts[:, s, :, 0, :],
                                ALU.subtract).then_inc(a_qkv, 1)
                v.wait_ge(a_qkv, q * 4 + 3)
                v.tensor_copy(parts[:, s, :, 1, :], rest[:, s, :, :]).then_inc(a_qkv, 1)
                v.wait_ge(a_qkv, q * 4 + 4)
                v.tensor_tensor(parts[:, s, :, 2, :], rest[:, s, :, :], parts[:, s, :, 1, :],
                                ALU.subtract).then_inc(a_parts, 1)
                v.wait_ge(a_parts, q + 1)
                for lo, n in ((0, 3), (3, 2), (5, 1)):
                    v.tensor_copy(stk[:, s, :, lo * QK:(lo + n) * QK].rearrange("p t (l c) -> p t l c", l=n),
                                  parts[:, s, :, 0:n, QK:2 * QK])
                for part, (lo, n) in enumerate(((0, 3), (3, 2), (5, 1))):
                    last = v.tensor_copy(stk[:, s, :, P + lo * QK:P + (lo + n) * QK].rearrange("p t (l c) -> p t l c", l=n),
                                         parts[:, s, :, part:part + 1, 0:QK].to_broadcast([P, TPC, n, QK]))
                last.then_inc(stk_ready, 1)

            def max_tile(gq, idx):
                t, c = divmod(idx, NCH)
                v.wait_ge(mx_ready, gq * (NMX + 1) + idx + 1)
                v.tensor_reduce(mxp[:, t, c:c + 1], ps[:, 4 + idx % 2, :], AX.X, ALU.max).then_inc(mx_free, 1)

            def max_parts(gq):
                v.wait_ge(mx_free, gq * MXC + NMX + 2)
                v.tensor_reduce(nm[:, :], mxp[:, :, :], AX.X, ALU.max, negate=True).then_inc(nm_step, 1)
                v.wait_ge(nm_step, gq * 5 + 1)
                v.tensor_copy(nms[:, :, 0], nm[:, :]).then_inc(nm_step, 1)
                v.wait_ge(nm_step, gq * 5 + 2)
                v.tensor_tensor(nmr[:, :], nm[:, :], nms[:, :, 0], ALU.subtract).then_inc(nm_step, 1)
                v.wait_ge(nm_step, gq * 5 + 3)
                v.tensor_copy(nms[:, :, 1], nmr[:, :]).then_inc(nm_step, 1)
                v.wait_ge(nm_step, gq * 5 + 4)
                v.tensor_tensor(nms[:, :, 2], nmr[:, :], nms[:, :, 1], ALU.subtract).then_inc(nm_step, 1)

            def max_rows(gq, g):
                v.wait_ge(mx_ready, (gq + 1) * (NMX + 1))
                v.tensor_copy(qs[NSTK:NROW, ds(g * CH, CH)], bank16(4, BF16)[0:3, 0:CH]).then_inc(mx_free, 2)

            def high_low(gq, i):
                n = gq * NU + i
                if i in DVE_HIGH:
                    v.wait_ge(exp_done, n + 3)
                    v.wait_ge(pv_done, n + 1)
                    v.tensor_copy(p_hi[:, i % RING, :], p32[:, i % RING, :]).then_inc(high_dve, 1)
                if i in DVE_LOW:
                    if i in DVE_HIGH:
                        v.wait_ge(high_dve, gq * len(DVE_HIGH) + (DVE_HIGH.index(i) + 1))
                    else:
                        v.wait_ge(high_act, gq * len(ACT_HIGH) + (ACT_HIGH.index(i) + 1))
                    v.tensor_tensor(p_lo[:, i % RING, :], p32[:, i % RING, :], p_hi[:, i % RING, :],
                                    ALU.subtract).then_inc(low_dve, 1)

            def finish_group(gq, g):
                v.wait_ge(acs_ready, (gq + 1) * 2)
                v.reciprocal(rsum[:, :], acs[:, :, PD]).then_inc(post, 1)
                v.tensor_tensor(attn[:, :, :], acs[:, :, 0:PD], acs[:, :, PD + 1:VN], ALU.add).then_inc(post, 1)
                v.wait_ge(post, gq * 5 + 2)
                v.scalar_tensor_tensor(attn[:, :, :], attn[:, :, :], 0.0,
                                       rsum[:, :].unsqueeze(2).to_broadcast([P, TPC, PD]),
                                       ALU.max, ALU.mult).then_inc(post, 1)
                v.wait_ge(post, gq * 5 + 3)
                at = ds(g * TPC, TPC)
                v.tensor_copy(xm_hi[:, at, 0:PD], attn[:, :, :]).then_inc(post, 1)
                v.wait_ge(post, gq * 5 + 4)
                v.tensor_tensor(xm_lo[:, at, 0:PD], attn[:, :, :], xm_hi[:, at, 0:PD], ALU.subtract).then_inc(post, 1)

            def group(gq, g, first, last_group):
                idx = 0
                for i in range(NU):
                    if not last_group:
                        for _ in range(MAX_AT[i]):
                            max_tile(gq + 1, idx)
                            idx += 1
                        if idx == NMX and MAX_AT[i]:
                            max_parts(gq + 1)
                    high_low(gq, i)
                    if i == MAX_ROWS_AT and not last_group:
                        max_rows(gq + 1, g + 1)
                    if i == 3 and not first:
                        finish_group(gq - 1, g - 1)

            def copy_turned(q):
                for k in range(KT):
                    v.wait_ge(xt_ready, q * KT + k + 1)
                    v.tensor_copy(xc[:, k, :, :].rearrange("p a n -> p (a n)"),
                                  bank16(2 + k % 2, F16)).then_inc(xt_copied, 1)

            def residual(b, jj, s, q):
                v.wait_ge(x_loaded[s], (b * NCH + jj + (NCH // 2 + 1)) * 16)
                for o in range(KT):
                    v.wait_ge(y_scaled, q * KT + o + 1)
                    v.tensor_tensor(x1[:, s, o, :], yb[:, o, :], xin[:, s, o, :], ALU.add).then_inc(x1_ready, 1)
                v.wait_ge(x1_ready, (q + 1) * KT)
                v.sem_inc(x_free, 1)

            def folded(q, s):
                for t in range(TPC):
                    v.wait_ge(u_ready, q * TPC + t + 1)
                    v.bn_stats(cst[:, s, t, :], ps[:, t % 2, 0:C]).then_inc(c_stat, 1)
                    v.tensor_copy(uraw[:, s, t, :], ps[:, t % 2, C:C + DR]).then_inc(u_taken, 1)
                v.wait_ge(c_stat, q * (TPC + 1) + TPC)
                v.sem_inc(passed, 1)
                for t in range(TPC):
                    last = v.bn_aggr(cmv[:, s, t, :], cst[:, s, t, :])
                last.then_inc(c_stat, 1)
                v.wait_ge(c_stat, q * (TPC + 1) + TPC + 1)
                v.tensor_scalar(cvar[:, s, :], cmv[:, s, :, 1], LN_FFN_EPS, None, ALU.add).then_inc(c_var, 1)

            def split_u(q, s):
                v.wait_ge(c_rstd, q + 1)
                v.wait_ge(u_taken, (q + 1) * TPC + 2)
                v.tensor_tensor(uf[:, s, :, :], uraw[:, s, :, :],
                                crstd[:, s, :].unsqueeze(2).to_broadcast([P, TPC, DR]), ALU.mult).then_inc(u_split, 1)
                v.wait_ge(u_split, q * 4 + 1)
                v.tensor_copy(us[:, s, :, 0:DR], uf[:, s, :, :]).then_inc(u_split, 1)
                v.tensor_copy(us[:, s, :, DR:2 * DR], uf[:, s, :, :]).then_inc(u_split, 1)
                v.wait_ge(u_split, q * 4 + 2)
                v.tensor_tensor(us[:, s, :, 2 * DR:3 * DR], uf[:, s, :, :], us[:, s, :, 0:DR],
                                ALU.subtract).then_inc(u_split, 1)
                v.wait_ge(ut_ready, q + 1)
                v.tensor_copy(uc[:, :], bank16(3, F16)[0:3 * DR, 0:CH]).then_inc(ut_copied, 1)

            def results(b, jj, s, q):
                v.wait_ge(z_ready, q + 1)
                v.tensor_copy(zs[:, :], ps[:, 2, :]).then_inc(z_copied, 1)
                v.wait_ge(stored[s], (b * (NCH // 2) + jj) * 16)
                for o in range(KT):
                    v.wait_ge(ff_ready, q * KT + o + 1)
                    v.tensor_tensor(outb[:, s, o, :], ps[:, 4 + o % 2, :], x1[:, s, o, :], ALU.add).then_inc(out_ready, 1)

            with v.Fori(0, B) as b:
                with v.Fori(0, NCH // 2) as jj:
                    for s in range(2):
                        q = b * NCH + jj * 2 + s
                        statistics(q, s)
                        v.sem_inc(x_free, 1)
                        qkv_parts(b, jj, s)
                gq0 = b * NCH
                for idx in range(NMX):
                    max_tile(gq0, idx)
                max_parts(gq0)
                max_rows(gq0, 0)
                group(gq0, 0, True, False)
                with v.Fori(1, NCH - 1) as g:
                    group(b * NCH + g, g, False, False)
                group(gq0 + (NCH - 1), NCH - 1, False, True)
                finish_group(gq0 + (NCH - 1), NCH - 1)
                with v.Fori(0, NCH // 2) as jj:
                    for s in range(2):
                        q = b * NCH + jj * 2 + s
                        copy_turned(q)
                        residual(b, jj, s, q)
                        folded(q, s)
                        split_u(q, s)
                        results(b, jj, s, q)

        @block.gpsimd
        def _(g):
            g.sem_inc(low_pool, len(POOL_LOW))
            g.wait_ge(bn_var_ready, 1)
            g.tensor_tensor(binv[:, :], bvar[:, :], expo[:, 0:4], ALU.pow).then_inc(set_pool, 1)
            g.wait_ge(norm_ready, 1)
            g.tensor_tensor(sc[:, 4:5], sc[:, 2:3], half[:, :], ALU.pow).then_inc(set_pool, 1)

            def chunk_a(b, jj, s):
                q = b * NCH + jj * 2 + s
                g.wait_ge(a_var, q + 1)
                g.tensor_tensor(rstd[:, s, :, :].rearrange("p a t -> p (a t)"),
                                var[:, s, :, :].rearrange("p a t -> p (a t)"), expo[:, :], ALU.pow).then_inc(a_rstd, 1)
                tiles = ds((jj * 2 + s) * TPC, TPC)
                g.wait_ge(v_hi, q + 1)
                g.tensor_tensor(vs[:, tiles, PD + 1:VN], qkvf[:, s, :, 2 * QK:], vs[:, tiles, 0:PD],
                                ALU.subtract).then_inc(v_lo, 1)
                g.wait_ge(skip_hi, q + 1)
                g.tensor_tensor(xm_lo[:, tiles, PD:C], skipf[:, s, :, :], xm_hi[:, tiles, PD:C],
                                ALU.subtract).then_inc(skip_lo, 1)

            def low_parts(gq):
                for i in POOL_LOW:
                    if i in DVE_HIGH:
                        g.wait_ge(high_dve, gq * len(DVE_HIGH) + (DVE_HIGH.index(i) + 1))
                    else:
                        g.wait_ge(high_act, gq * len(ACT_HIGH) + (ACT_HIGH.index(i) + 1))
                    g.tensor_tensor(p_lo[:, i % RING, :], p32[:, i % RING, :], p_hi[:, i % RING, :],
                                    ALU.subtract).then_inc(low_pool, 1)

            with g.Fori(0, B) as b:
                with g.Fori(0, NCH // 2) as jj:
                    for s in range(2):
                        chunk_a(b, jj, s)
                with g.Fori(0, NCH) as gr:
                    low_parts(b * NCH + gr)
                with g.Fori(0, NCH // 2) as jj:
                    for s in range(2):
                        q = b * NCH + jj * 2 + s
                        g.wait_ge(c_var, q + 1)
                        g.tensor_tensor(crstd[:, s, :], cvar[:, s, :], expo[:, 0:TPC], ALU.pow).then_inc(c_rstd, 1)


_INS = {"x": "x", "L0_conv_ln_w": "ln_w", "L0_conv_ln_b": "ln_b", "L0_conv_w_qkv": "w_qkv",
        "L0_conv_bn1_g": "bn1_g", "L0_conv_bn1_b": "bn1_b", "L0_conv_bn1_m": "bn1_m", "L0_conv_bn1_v": "bn1_v",
        "L0_conv_w_proj": "w_proj", "L0_conv_bn2_g": "bn2_g", "L0_conv_bn2_b": "bn2_b", "L0_conv_bn2_m": "bn2_m",
        "L0_conv_bn2_v": "bn2_v", "L0_ffn_c_fc_1": "c_fc_1", "L0_ffn_c_fc_2": "c_fc_2",
        "L0_ffn_c_proj_1": "c_proj_1", "L0_ffn_c_proj_2": "c_proj_2"}


def shape_constants():
    ch = np.arange(C)
    blk = (ch[:, None] // DB == np.arange(DR)[None, :]).astype(np.float32)
    return {
        "ident": np.eye(P, dtype=np.float32),
        "rep": (ch[None, :] % DB == np.arange(DB)[:, None]).astype(np.float32),
        "blk": blk,
        "blkt": np.ascontiguousarray(np.concatenate([blk.T] * 4, axis=0)),
    }


def kernel(**inputs):
    import concourse.bacc as bacc
    from concourse.bass_utils import run_bass_kernel_spmd

    nc = bacc.Bacc("TRN2", target_bir_lowering=False, num_devices=1)
    arrays, aps = {}, {}
    for name, short in _INS.items():
        arrays[f"in_{short}"] = np.ascontiguousarray(inputs[name])
    for short, a in shape_constants().items():
        arrays[f"in_{short}"] = a
    for key, a in arrays.items():
        aps[key[3:]] = nc.dram_tensor(key, a.shape, mybir.dt.from_np(a.dtype), kind="ExternalInput").ap()
    aps["out"] = nc.dram_tensor("out_0", (B, C, H, W), F32, kind="ExternalOutput").ap()
    build(nc, aps)
    r = run_bass_kernel_spmd(nc, [arrays], core_ids=[0])
    return r.results[0]["out_0"]
```

```python
from contextlib import ExitStack

import numpy as np
import concourse.bass as bass
from concourse import mybir

F32, F16, BF16 = mybir.dt.float32, mybir.dt.float16, mybir.dt.bfloat16
ALU = mybir.AluOpType
ACT = mybir.ActivationFunctionType
AX = mybir.AxisListType
ds = bass.ds

B, C, H, W = 4, 384, 64, 64
N = H * W
P = 128
PD, QK = 96, 16
QKV = 2 * QK + PD
KT = C // P
CH = 512
NCH = N // CH
TPC = CH // P
NA = NCH // 2
NT = N // P
DFF, DR, DB = 1536, 32, 12
JT = DFF // P
SK = C - PD
NSTK = 6 * QK
NROW = NSTK + 3
VP = 2 * PD + 2
VN = 2 * PD + 1
KPU = 2
NU = NT // KPU
UW = KPU * CH
RING = 4

LN_IN_EPS, LN_ATTN_EPS, LN_FFN_EPS, BN_EPS = 1e-6, 1e-5, 1e-5, 1e-5
F16_TOP = 2.0 ** 14
SKIP_SCALE = 2.0 ** 9
U_SCALE = 2.0 ** 9
W_TOP = 2.0 ** 12
TINY = 1e-30
SCALE = QK ** -0.5
EXP_SHIFT = 10 / SCALE

POOL_LOW = tuple(i for i in range(NU) if i not in (2, 7, 12))
DVE_HIGH = (2, 7, 12)
DVE_LOW = tuple(i for i in range(NU) if i not in POOL_LOW)
ACT_HIGH = tuple(i for i in range(NU) if i not in DVE_HIGH)
NMX = TPC * NCH
LEAD = 3
MAX_AT = [2, 3, 2, 2, 2, 2, 3, 2, 2, 2, 2, 0, 2, 2, 2, 2]
MAX_ROWS_AT = 11
FINISH_AT = (3, 5, 8, 9)
MAX_EARLY = sum(MAX_AT[MAX_ROWS_AT:])
assert sum(MAX_AT) == NMX
N_LOADS = 20
MXC = NMX + 2


def max_tiles_at(i):
    first = sum(MAX_AT[MAX_ROWS_AT:i]) if i >= MAX_ROWS_AT else MAX_EARLY + sum(MAX_AT[:i])
    return range(first, first + MAX_AT[i])


def build(nc, A):
    ctx = ExitStack()
    with ctx:
        def sb(name, shape, dt=F32):
            return ctx.enter_context(nc.sbuf_tensor(name, shape, dt))

        def sem(name):
            return ctx.enter_context(nc.semaphore(name))

        ident = sb("ident", [P, P])
        ident_h = sb("ident_h", [P, P], F16)
        ident_b = sb("ident_b", [P, P], BF16)
        ones = sb("ones", [P, P])
        expo = sb("expo", [P, 8])
        half = sb("half", [P, 1])
        w_qkv = sb("w_qkv", [PD, QKV])
        bias_qkv = sb("bias_qkv", [P, QKV])
        wp_hi = sb("wp_hi", [P, KT, C], F16)
        wp_lo = sb("wp_lo", [P, KT, C], F16)
        wp_unscale = sb("wp_unscale", [P, KT])
        shift2 = sb("shift2", [P, KT])
        fold = sb("fold", [P, KT, DR])
        fc1 = sb("fc1", [3 * DR, DFF], F16)
        gelu_scale = sb("gelu_scale", [P, JT])
        p1t = sb("p1t", [P, JT, DR])
        spread = sb("spread", [P, C])
        ks = sb("ks", [P, N], BF16)
        qs = sb("qs", [P, N], BF16)
        vs = sb("vs", [P, NT, VP], F16)
        xm_hi = sb("xm_hi", [P, NT, C], F16)
        xm_lo = sb("xm_lo", [P, NT, C], F16)
        xin = sb("xin", [P, 2, KT, CH])
        pool32 = sb("pool32", [P, 8192])
        p32 = pool32[:, 0:RING * UW].rearrange("p (r n) -> p r n", r=RING)
        p_hi = pool32[:, 4096:6144].bitcast(F16).rearrange("p (r n) -> p r n", r=RING)
        p_lo = pool32[:, 6144:8192].bitcast(F16).rearrange("p (r n) -> p r n", r=RING)
        gel = pool32[:, 0:JT * CH].rearrange("p (j n) -> p j n", j=JT)
        xt = sb("xt", [P, 2, TPC, C + QKV])
        qkvf = sb("qkvf", [P, 2, TPC, QKV])
        rest = sb("rest", [P, 2, TPC, 2 * QK])
        parts = sb("parts", [P, 2, TPC, 3, 2 * QK], BF16)
        stk = sb("stk", [P, 2, TPC, 2 * P], BF16)
        bst = sb("bst", [P, 2, TPC, 2, 6])
        mv = sb("mv", [P, 2, TPC, 2, 2])
        var = sb("var", [P, 2, 2, TPC])
        rstd = sb("rstd", [P, 2, 2, TPC])
        skip_s = sb("skip_s", [P, 2, TPC])
        skip_b = sb("skip_b", [P, 2, TPC])
        mxp = sb("mxp", [P, TPC, NCH])
        nm = sb("nm", [P, TPC])
        nmr = sb("nmr", [P, TPC])
        nms = sb("nms", [P, TPC, 3], BF16)
        acs = sb("acs", [P, TPC, VP])
        attn = sb("attn", [P, TPC, PD])
        rsum = sb("rsum", [P, TPC])
        xc = sb("xc", [P, KT, 2, CH], F16)
        yb = sb("yb", [P, KT, CH])
        x1 = sb("x1", [P, 2, KT, CH])
        cst = sb("cst", [P, 2, TPC, 6])
        cmv = sb("cmv", [P, 2, TPC, 2])
        cvar = sb("cvar", [P, 2, TPC])
        crstd = sb("crstd", [P, 2, TPC])
        uraw = sb("uraw", [P, 2, TPC, DR])
        uf = sb("uf", [P, 2, TPC, DR])
        us = sb("us", [P, 2, TPC, 3 * DR], F16)
        uc = sb("uc", [3 * DR, CH], F16)
        zs = sb("zs", [P, CH])
        raw_qkv = sb("raw_qkv", [P, PD])
        lnw = sb("lnw", [P, PD])
        lnb = sb("lnb", [P, PD])
        bn1 = sb("bn1", [P, 4])
        bn2 = sb("bn2", [P, 4, KT])
        bvar = sb("bvar", [P, 4])
        binv = sb("binv", [P, 4])
        sc = sb("sc", [P, 16])
        diag = sb("diag", [P, P])
        fccol = sb("fccol", [DB, 4])
        rep = sb("rep", [DB, C])
        p2b = sb("p2b", [DB, P])
        blk = sb("blk", [P, KT, DR])
        blkt = sb("blkt", [P, C])
        fmax = sb("fmax", [P, JT])
        fsig = sb("fsig", [P, JT])
        wmax = sb("wmax", [P, KT])
        raw_p = pool32[:, 0:1152].rearrange("p (t n) -> p t n", t=KT)
        wph0 = pool32[:, 1152:1728].bitcast(F16).rearrange("p (t n) -> p t n", t=KT)
        wpl0 = pool32[:, 1728:2304].bitcast(F16).rearrange("p (t n) -> p t n", t=KT)
        colscale = pool32[:, 2304:2688]
        raw_f = pool32[:, 2688:3072].rearrange("p (j n) -> p j n", j=JT)
        fstk = pool32[:, 3072:3648].bitcast(F16).rearrange("p (j n) -> p j n", j=JT)
        raw_p1 = pool32[0:DR, 3648:5184]
        w1 = pool32[:, 5184:5280]
        junk = pool32[:, 5280:5376]

        ps = ctx.enter_context(nc.psum_tensor("ps", [P, 8, 512], F32))

        def bank16(b, dt):
            return ps[:, b, :].bitcast(dt)

        w_loaded = sem("w_loaded")
        set_dve = sem("set_dve")
        set_pe = sem("set_pe")
        set_pool = sem("set_pool")
        bn_var_ready = sem("bn_var_ready")
        norm_ready = sem("norm_ready")
        w1_ready = sem("w1_ready")
        tau_ready = sem("tau_ready")
        wp_ready = sem("wp_ready")
        set_up = sem("set_up")
        x_loaded = [sem("x_loaded0"), sem("x_loaded1")]
        x_free = [sem("x_free0"), sem("x_free1")]
        tok_ready = sem("tok_ready")
        tok_taken = sem("tok_taken")
        a_stat = sem("a_stat")
        a_var = sem("a_var")
        a_rstd = sem("a_rstd")
        a_skip = sem("a_skip")
        a_parts = sem("a_parts")
        a_qkv = sem("a_qkv")
        stk_ready = sem("stk_ready")
        stk_turned = sem("stk_turned")
        stk_copied = sem("stk_copied")
        skip_f = sem("skip_f")
        skip_hi = sem("skip_hi")
        skip_lo = sem("skip_lo")
        v_hi = sem("v_hi")
        v_lo = sem("v_lo")
        st_ready = sem("st_ready")
        exp_done = sem("exp_done")
        high_act = sem("high_act")
        high_dve = sem("high_dve")
        low_dve = sem("low_dve")
        low_pool = sem("low_pool")
        pv_done = sem("pv_done")
        mx_ready = sem("mx_ready")
        mx_free = sem("mx_free")
        nm_step = sem("nm_step")
        acs_ready = sem("acs_ready")
        passed = sem("passed")
        post = sem("post")
        xt_ready = sem("xt_ready")
        xt_copied = sem("xt_copied")
        y_ready = sem("y_ready")
        y_scaled = sem("y_scaled")
        x1_ready = sem("x1_ready")
        u_ready = sem("u_ready")
        u_taken = sem("u_taken")
        c_stat = sem("c_stat")
        c_var = sem("c_var")
        c_rstd = sem("c_rstd")
        u_split = sem("u_split")
        ut_ready = sem("ut_ready")
        ut_copied = sem("ut_copied")
        h_ready = sem("h_ready")
        g_ready = sem("g_ready")
        z_ready = sem("z_ready")
        z_copied = sem("z_copied")
        ff_ready = sem("ff_ready")
        out_ready = sem("out_ready")
        stored = [sem("stored0"), sem("stored1")]

        x_v = A["x"].rearrange("b (k p) h w -> p b k (h w)", p=P)
        out_v = A["out"].rearrange("b (k p) h w -> p b k (h w)", p=P)

        block = ctx.enter_context(nc.Block())

        @block.sync
        def _(sp):
            def col(v):
                return v.rearrange("(p o) -> p o", o=1)

            loads = [
                (ident[:, :], A["ident"]), (rep[:, :], A["rep"]),
                (blk[:, :, :], A["blk"].rearrange("(k p) a -> p k a", p=P)), (blkt[:, :], A["blkt"]),
                (raw_qkv[:, :], A["w_qkv"]),
                (lnw[:, :], A["ln_w"].partition_broadcast(P)), (lnb[:, :], A["ln_b"].partition_broadcast(P)),
                (bn1[:, 0:1], col(A["bn1_g"])), (bn1[:, 1:2], col(A["bn1_b"])),
                (bn1[:, 2:3], col(A["bn1_m"])), (bn1[:, 3:4], col(A["bn1_v"])),
                (bn2[:, 0, :], A["bn2_g"].rearrange("(k p) -> p k", p=P)),
                (bn2[:, 1, :], A["bn2_b"].rearrange("(k p) -> p k", p=P)),
                (bn2[:, 2, :], A["bn2_m"].rearrange("(k p) -> p k", p=P)),
                (bn2[:, 3, :], A["bn2_v"].rearrange("(k p) -> p k", p=P)),
                (raw_p, A["w_proj"].rearrange("(k p) c -> p k c", p=P)),
                (raw_f, A["c_fc_1"].rearrange("(j p) a -> p j a", p=P)),
                (raw_p1, A["c_proj_1"]),
                (fccol[:, 0:1], A["c_fc_2"].rearrange("a b -> b a")), (fccol[:, 1:2], A["c_proj_2"]),
            ]
            assert len(loads) == N_LOADS
            with nc.allow_non_contiguous_dma(reason="small vectors, once"):
                for dst, src in loads:
                    sp.dma_start(dst, src).then_inc(w_loaded, 16)

            def load_x(b, j, s, n):
                sp.wait_ge(x_free[s], n + 1)
                src = x_v[:, ds(b, 1), :, ds(j * CH, CH)].rearrange("p o k n -> p (o k) n")
                sp.dma_start(xin[:, s, :, :], src).then_inc(x_loaded[s], 16)

            def store(b, j, s):
                sp.wait_ge(out_ready, (b * NCH + j + 1) * KT)
                dst = out_v[:, ds(b, 1), :, ds(j * CH, CH)].rearrange("p o k n -> p (o k) n")
                sp.dma_start(dst, x1[:, s, :, :]).then_inc(stored[s], 16)

            def phase_c(b, with_next):
                load_x(b, 0, 0, b * NCH + NA)
                if with_next:
                    load_x(b + 1, 0, 1, b * NCH + NA)
                load_x(b, 1, 0, b * NCH + (NA + 1))

                def chunk(j, s, late):
                    if with_next and late > 0:
                        load_x(b + 1, j + 1, 1, b * NCH + (NA + 1) + j)
                    if late > 1:
                        load_x(b, j + 2, 0, b * NCH + (NA + 2) + j)
                    store(b, j, s)

                with sp.Fori(0, NCH // 2 - 1) as jj:
                    for s in range(2):
                        chunk(jj * 2 + s, s, 2)
                chunk(NCH - 2, 0, 1)
                chunk(NCH - 1, 1, 0)

            with sp.Fori(0, NA) as jj:
                for s in range(2):
                    load_x(0, jj * 2 + s, s, jj)
            with sp.Fori(0, B - 1) as b:
                phase_c(b, True)
            phase_c(B - 1, False)
            for s in range(2):
                sp.wait_ge(stored[s], 16 * B * NCH // 2)

        @block.tensor
        def _(pe):
            mm = pe.matmul

            pe.wait_ge(w1_ready, 1)
            pe.transpose(ps[0:PD, 0, 0:P], w1, ident[:, :])
            mm(ps[:, 1, 0:P], ones[:, :], diag[:, :], start=True, stop=True).then_inc(set_pe, 1)
            pe.wait_ge(tau_ready, 1)
            mm(ps[:, 2, 0:PD], ones[:, :], diag[:, 2 * QK:], start=True, stop=True).then_inc(set_pe, 1)
            mm(ps[:, 3, 0:1], ones[0:DB, :], fccol[:, 0:1], start=True, stop=True)
            mm(ps[:, 3, 1:2], ones[0:DB, :], fccol[:, 2:3], start=True, stop=True)
            for k in range(KT):
                mm(ps[:, 3, 2 + k:3 + k], rep[:, k * P:(k + 1) * P], fccol[:, 0:1], start=True, stop=True)
            mm(ps[:, 4, 0:C], p2b[:, :], rep[:, :], start=True, stop=True).then_inc(set_pe, 1)
            for j in range(JT):
                last = pe.transpose(ps[:, 5, j * DR:(j + 1) * DR], raw_p1[:, j * P:(j + 1) * P], ident[0:DR, 0:DR])
            last.then_inc(set_pe, 1)
            pe.wait_ge(wp_ready, 1)
            for k in range(KT):
                for part, src in ((0, wph0), (1, wpl0)):
                    for o in range(KT):
                        last = pe.transpose(bank16((6, 7, 0)[k], F16)[:, part * 512 + o * P:part * 512 + (o + 1) * P],
                                            src[:, o, k * P:(k + 1) * P], ident_h[:, :])
            for j in range(JT):
                last = pe.transpose(bank16(1 + j // 8, F16)[0:3 * DR, (j % 8) * P:(j % 8 + 1) * P],
                                    fstk[:, j, :], ident_h[:, :])
            last.then_inc(set_pe, 1)
            pe.wait_ge(set_up, 1)

            def tokens(qa, buf, s, loads, after_u=None):
                pe.wait_ge(x_loaded[buf], loads * 16)
                for t in range(TPC):
                    if t >= 2:
                        pe.wait_ge(tok_taken, qa * TPC + t - 1)
                    elif after_u is not None:
                        pe.wait_ge(u_taken, after_u * TPC + t + 3)
                    else:
                        pe.wait_ge(tok_taken, qa * TPC)
                    bk = ps[:, t % 2, :]
                    for k in range(KT):
                        pe.transpose(bk[:, k * P:(k + 1) * P], xin[:, buf, k, t * P:(t + 1) * P], ident[:, :])
                    mm(bk[:, C:C + QKV], xin[0:PD, buf, 0, t * P:(t + 1) * P], w_qkv[:, :],
                       start=True, stop=True).then_inc(tok_ready, 1)

            def turn_stacks(qa, s, bank):
                pe.wait_ge(stk_ready, qa + 1)
                pe.wait_ge(stk_copied, qa)
                pe.wait_ge(tok_taken, (qa + 1) * TPC)
                bk = bank16(bank, BF16)
                for t in range(TPC):
                    pe.transpose(bk[0:NROW, t * P:(t + 1) * P], stk[:, s, t, 0:NROW], ident_b[:, :])
                    last = pe.transpose(bk[0:NSTK, CH + t * P:CH + (t + 1) * P], stk[:, s, t, P:P + NSTK], ident_b[:, :])
                last.then_inc(stk_turned, 1)

            def max_tile(gq, g, idx):
                t, c = divmod(idx, NCH)
                pe.wait_ge(mx_free, gq * MXC + idx + 1)
                mm(ps[:, 4 + idx % 2, :], qs[0:NSTK, ds(g * CH + t * P, P)], ks[0:NSTK, c * CH:(c + 1) * CH],
                   start=True, stop=True).then_inc(mx_ready, 1)

            def max_rows(gq):
                pe.wait_ge(mx_free, gq * MXC + NMX + 1)
                pe.wait_ge(nm_step, (gq + 1) * 6)
                for t in range(TPC):
                    last = pe.transpose(bank16(4, BF16)[0:3, t * P:(t + 1) * P], nms[:, t, :], ident_b[:, :])
                last.then_inc(mx_ready, 1)

            def scores(gq, g, i):
                n = gq * NU + i
                if i == 0:
                    pe.wait_ge(mx_free, (gq + 1) * MXC + 2)
                pe.wait_ge(exp_done, n + 1)
                for h in range(KPU):
                    kt = KPU * i + h
                    last = mm(ps[:, 2 * (i % 2) + h, :], ks[0:NROW, kt * P:(kt + 1) * P], qs[0:NROW, ds(g * CH, CH)],
                              start=True, stop=True)
                last.then_inc(st_ready, 1)

            def values(gq, i, between=None):
                if i in POOL_LOW:
                    pe.wait_ge(low_pool, (gq + 1) * len(POOL_LOW) + (POOL_LOW.index(i) + 1))
                else:
                    pe.wait_ge(low_dve, (gq + 1) * len(DVE_LOW) + (DVE_LOW.index(i) + 1))
                if i == 0:
                    pe.wait_ge(acs_ready, gq * 2 + 0)
                for h in range(KPU):
                    if h == 1 and between:
                        between()
                    kt = KPU * i + h
                    for t in range(TPC):
                        acc = ps[:, 6 + t // 2, (t % 2) * VP:(t % 2) * VP + VN]
                        at = h * CH + t * P
                        mm(acc, p_hi[:, i % RING, at:at + P], vs[:, kt, 0:VN],
                           start=(kt == 0 and t % 2 == 0), stop=False, skip_group_check=True)
                        last = mm(acc[:, 0:PD + 1], p_lo[:, i % RING, at:at + P], vs[:, kt, 0:PD + 1],
                                  start=False, stop=(kt == NT - 1), skip_group_check=True)
                last.then_inc(pv_done, 1)

            def group(gq, g, left):
                for i in range(NU):
                    tiles = list(max_tiles_at(i))

                    def next_max():
                        if tiles and i < MAX_ROWS_AT and left >= 1:
                            max_tile(gq + 1, g + 1, tiles.pop(0))
                        if tiles and i > MAX_ROWS_AT and left >= 2:
                            max_tile(gq + 2, g + 2, tiles.pop(0))

                    next_max()
                    if i + LEAD < NU:
                        scores(gq, g, i + LEAD)
                    elif left >= 1:
                        scores(gq + 1, g + 1, i + LEAD - NU)
                    next_max()
                    values(gq, i, next_max)
                    if i == MAX_ROWS_AT and left >= 1:
                        max_rows(gq + 1)

            def turn_input(j, q, k):
                if k == 0:
                    pe.wait_ge(post, (q + 1) * 5)
                    pe.wait_ge(skip_lo, q + 2)
                if k == 1:
                    pe.wait_ge(z_copied, q - z_lag[0])
                if k == 2:
                    pe.wait_ge(xt_copied, q * KT + 1)
                bk = bank16(2 + k % 2, F16)
                for part, src in ((0, xm_hi), (1, xm_lo)):
                    for t in range(TPC):
                        last = pe.transpose(bk[:, part * CH + t * P:part * CH + (t + 1) * P],
                                            src[:, ds(j * TPC + t, 1), k * P:(k + 1) * P].rearrange("p o n -> p (o n)"),
                                            ident_h[:, :])
                last.then_inc(xt_ready, 1)

            def project(q, o, outs):
                bk = ps[:, 4 + o % 2, :]
                terms = [(w, k, part) for k in range(KT) for w, part in ((wp_hi, 0), (wp_lo, 0), (wp_hi, 1))]
                for n, (w, k, part) in enumerate(terms):
                    if n == 0:
                        pe.wait_ge(xt_copied, (q + 1) * KT)
                        if o == 2:
                            pe.wait_ge(y_scaled, q * KT + 1)
                        else:
                            pe.wait_ge(out_ready, outs * KT)
                    last = mm(bk, w[:, k, o * P:(o + 1) * P], xc[:, k, part, :], start=(n == 0), stop=(n == len(terms) - 1))
                    if n == len(terms) - 1:
                        last.then_inc(y_ready, 1)
                    yield

            def fold_u(q, s, stacks):
                pe.wait_ge(x1_ready, (q + 1) * KT)
                for t in range(TPC):
                    if t < 2:
                        pe.wait_ge(stk_copied, stacks)
                        pe.wait_ge(u_taken, q * TPC)
                    else:
                        pe.wait_ge(u_taken, q * TPC + t - 1)
                    bk = ps[:, t % 2, :]
                    for k in range(KT):
                        pe.transpose(bk[:, k * P:(k + 1) * P], x1[:, s, k, t * P:(t + 1) * P], ident[:, :])
                    for k in range(KT):
                        last = mm(bk[:, C:C + DR], x1[:, s, k, t * P:(t + 1) * P], fold[:, k, :],
                                  start=(k == 0), stop=(k == KT - 1), skip_group_check=True)
                    last.then_inc(u_ready, 1)

            def turn_u(q, s):
                pe.wait_ge(u_split, (q + 1) * 4)
                for t in range(TPC):
                    last = pe.transpose(bank16(3, F16)[0:3 * DR, t * P:(t + 1) * P], us[:, s, t, :], ident_h[:, :])
                last.then_inc(ut_ready, 1)
                pe.wait_ge(ut_copied, q + 1)

            def up(q, j):
                pe.wait_ge(g_ready, q * JT + j + 1)
                mm(ps[:, 6 + j % 2, :], fc1[:, j * P:(j + 1) * P], uc[:, :], start=True, stop=True).then_inc(h_ready, 1)

            def down(q, r):
                pe.wait_ge(g_ready, q * JT + 4 * r + 4 + 2)
                for c in range(4):
                    last = mm(ps[c * DR:(c + 1) * DR, 3, :], p1t[:, 4 * r + c, :], gel[:, 4 * r + c, :],
                              start=(r == 0), stop=(r == JT // 4 - 1), tile_position=(0, c * DR))
                if r == JT // 4 - 1:
                    last.then_inc(z_ready, 1)

            def expand(q, scaled):
                pe.wait_ge(z_copied, q + 1)
                pe.wait_ge(y_scaled, scaled)
                for o in range(KT):
                    if o == 2:
                        pe.wait_ge(out_ready, q * KT + 1)
                    mm(ps[:, 5 - o % 2, :], spread[:, o * P:(o + 1) * P], zs[:, :], start=True, stop=True).then_inc(ff_ready, 1)

            def chunk_c(b, j, s, late, with_next):
                q = b * NCH + j
                qa = q + NCH
                fold_u(q, s, qa if with_next else B * NCH)
                if with_next:
                    tokens(qa, 1, s, b * NCH + j + (NA + 1), after_u=q)
                work = []
                if late >= 1:
                    for _ in project(q + 1, 0, q):
                        pass
                    work = [project(q + 1, 1, q), project(q + 1, 2, q)]
                turn_u(q, s)
                for n in range(JT):
                    up(q, n)
                    for _ in range(1 + n % 2):
                        if work and next(work[0], "end") == "end":
                            work.pop(0)
                            if work:
                                next(work[0])
                    if n == 5:
                        down(q, 0)
                    if n == 9:
                        down(q, 1)
                for w in work:
                    for _ in w:
                        pass
                down(q, 2)
                if late >= 2:
                    turn_input(j + 2, q + 2, 0)
                if with_next:
                    turn_stacks(qa, s, 0)
                expand(q, (q + (2 if late >= 1 else 1)) * KT)
                if late >= 2:
                    turn_input(j + 2, q + 2, 1)
                    turn_input(j + 2, q + 2, 2)

            z_lag = [0]

            def phase_c(b, with_next):
                q0 = b * NCH
                pe.wait_ge(acs_ready, (q0 + NCH) * 2)
                for j in range(2):
                    z_lag[0] = j
                    for k in range(KT):
                        turn_input(j, q0 + j, k)
                    if j == 0:
                        for o in range(KT):
                            for _ in project(q0, o, q0):
                                pass
                z_lag[0] = 1
                with pe.Fori(0, NCH // 2 - 1) as jj:
                    for s in range(2):
                        chunk_c(b, jj * 2 + s, s, 2, with_next)
                chunk_c(b, NCH - 2, 0, 1, with_next)
                chunk_c(b, NCH - 1, 1, 0, with_next)

            def phase_b(b):
                gq0 = b * NCH
                pe.wait_ge(out_ready, b * (NCH * KT))
                pe.wait_ge(stk_copied, gq0 + NCH)
                pe.wait_ge(v_lo, gq0 + NCH + 1)
                for idx in range(NMX):
                    max_tile(gq0, 0, idx)
                max_rows(gq0)
                for idx in range(MAX_EARLY):
                    max_tile(gq0 + 1, 1, idx)
                for i in range(LEAD):
                    scores(gq0, 0, i)
                with pe.Fori(0, NCH - 2) as g:
                    group(b * NCH + g, g, 2)
                group(gq0 + (NCH - 2), NCH - 2, 1)
                group(gq0 + (NCH - 1), NCH - 1, 0)

            with pe.Fori(0, NA) as jj:
                for s in range(2):
                    tokens(jj * 2 + s, s, s, jj + 1)
                    turn_stacks(jj * 2 + s, s, 2)
            with pe.Fori(0, B - 1) as b:
                phase_b(b)
                phase_c(b, True)
            phase_b(B - 1)
            phase_c(B - 1, False)

        @block.scalar
        def _(act):
            act.sem_inc(exp_done, 2)
            act.sem_inc(g_ready, 2)

            def take_tokens(qa, s):
                act.wait_ge(skip_lo, qa)
                for t in range(TPC):
                    act.wait_ge(tok_ready, qa * TPC + t + 1)
                    act.activation(xt[:, s, t, :], ps[:, t % 2, :], ACT.Copy).then_inc(tok_taken, 1)

            def skip_values(qa, j, s):
                act.wait_ge(a_qkv, qa * 4 + 1)
                for t in range(TPC):
                    last = act.activation(xt[:, s, t, PD:C], xt[:, s, t, PD:C], ACT.Relu,
                                          bias=skip_b[:, s, t:t + 1], scale=skip_s[:, s, t:t + 1])
                last.then_inc(skip_f, 1)
                act.wait_ge(skip_f, qa + 1)
                act.activation(xm_hi[:, ds(j * TPC, TPC), PD:C], xt[:, s, :, PD:C], ACT.Copy).then_inc(skip_hi, 1)

            def copy_stacks(qa, j, bank):
                act.wait_ge(stk_turned, qa + 1)
                src = bank16(bank, BF16)
                act.activation(ks[0:NROW, ds(j * CH, CH)], src[0:NROW, 0:CH], ACT.Copy)
                act.activation(qs[0:NSTK, ds(j * CH, CH)], src[0:NSTK, CH:2 * CH], ACT.Copy).then_inc(stk_copied, 1)

            def exponentials(gq, i):
                n = gq * NU + i
                j = (i - RING) % NU
                if j in POOL_LOW:
                    act.wait_ge(low_pool, (gq + (1 if i >= RING else 0)) * len(POOL_LOW) + (POOL_LOW.index(j) + 1))
                else:
                    act.wait_ge(low_dve, (gq + (1 if i >= RING else 0)) * len(DVE_LOW) + (DVE_LOW.index(j) + 1))
                act.wait_ge(st_ready, n + 1)
                act.activation(p32[:, i % RING, :].rearrange("p (h n) -> p h n", h=KPU),
                               ps[:, 2 * (i % 2):2 * (i % 2) + 2, :], ACT.Exp,
                               scale=SCALE).then_inc(exp_done, 1)

            def high(gq, i):
                if i not in ACT_HIGH:
                    return
                n = gq * NU + i
                act.wait_ge(exp_done, n + 3)
                act.wait_ge(pv_done, n + 1)
                act.activation(p_hi[:, i % RING, :], p32[:, i % RING, :], ACT.Copy).then_inc(high_act, 1)

            def group(gq):
                for i in range(NU):
                    exponentials(gq, i)
                    high(gq, i)

            def project_out(q, o):
                act.wait_ge(y_ready, q * KT + o + 1)
                act.wait_ge(x1_ready, q * KT)
                act.activation(yb[:, o, :], ps[:, 4 + o % 2, :], ACT.Identity,
                               bias=shift2[:, o:o + 1], scale=wp_unscale[:, o:o + 1]).then_inc(y_scaled, 1)

            def gelu(q, j):
                act.wait_ge(h_ready, q * JT + j + 1)
                act.activation(gel[:, j, :], ps[:, 6 + j % 2, :], ACT.Gelu,
                               scale=gelu_scale[:, j:j + 1]).then_inc(g_ready, 1)

            def chunk_c(b, j, s, late, with_next):
                q = b * NCH + j
                qa = q + NCH
                if with_next:
                    take_tokens(qa, s)
                if late >= 1:
                    project_out(q + 1, 0)
                act.wait_ge(z_ready, q)
                for n in range(JT):
                    gelu(q, n)
                    if late >= 1 and n == 6:
                        project_out(q + 1, 1)
                if late >= 1:
                    project_out(q + 1, 2)
                if with_next:
                    skip_values(qa, j, s)
                    copy_stacks(qa, j, 0)

            def phase_c(b, with_next):
                for o in range(KT):
                    project_out(b * NCH, o)
                with act.Fori(0, NCH // 2 - 1) as jj:
                    for s in range(2):
                        chunk_c(b, jj * 2 + s, s, 2, with_next)
                chunk_c(b, NCH - 2, 0, 1, with_next)
                chunk_c(b, NCH - 1, 1, 0, with_next)

            def phase_b(b):
                with act.Fori(0, NCH) as g:
                    group(b * NCH + g)

            act.wait_ge(set_up, 1)
            with act.Fori(0, NA) as jj:
                for s in range(2):
                    j = jj * 2 + s
                    take_tokens(j, s)
                    skip_values(j, j, s)
                    copy_stacks(j, j, 2)
            with act.Fori(0, B - 1) as b:
                phase_b(b)
                phase_c(b, True)
            phase_b(B - 1)
            phase_c(B - 1, False)

        @block.vector
        def _(v):
            v.sem_inc(x_free[0], 1)
            v.sem_inc(x_free[1], 1)
            v.sem_inc(mx_free, 2)
            v.sem_inc(low_dve, len(DVE_LOW))
            v.sem_inc(pv_done, RING)
            steps = [0]

            def link(ins):
                steps[0] += 1
                ins.then_inc(set_dve, 1)
                v.wait_ge(set_dve, steps[0])

            link(v.memset(ones[:, :], 1.0))
            link(v.memset(expo[:, :], -0.5))
            link(v.memset(half[:, :], 0.5))
            link(v.memset(stk[:, :, :, :], 1.0))
            link(v.memset(vs[:, :, :], 1.0))
            v.wait_ge(w_loaded, 16 * N_LOADS)
            link(v.tensor_copy(ident_h[:, :], ident[:, :]))
            link(v.tensor_copy(ident_b[:, :], ident[:, :]))
            link(v.tensor_scalar(bvar[:, 0:1], bn1[:, 3:4], BN_EPS, None, ALU.add))
            link(v.tensor_scalar(bvar[:, 1:4], bn2[:, 3, :], BN_EPS, None, ALU.add))
            v.sem_inc(bn_var_ready, 1)
            v.wait_ge(set_pool, 1)
            link(v.tensor_tensor(binv[:, 0:1], binv[:, 0:1], bn1[:, 0:1], ALU.mult))
            link(v.tensor_tensor(binv[:, 1:4], binv[:, 1:4], bn2[:, 0, :], ALU.mult))
            link(v.tensor_tensor(junk, raw_qkv[:, :], lnb[:, :], ALU.mult))
            link(v.tensor_reduce(sc[:, 0:1], junk, AX.X, ALU.add))
            link(v.tensor_tensor(sc[:, 0:1], sc[:, 0:1], bn1[:, 2:3], ALU.subtract))
            link(v.scalar_tensor_tensor(sc[:, 0:1], sc[:, 0:1], binv[:, 0:1], bn1[:, 1:2], ALU.mult, ALU.add))
            link(v.scalar_tensor_tensor(w1, raw_qkv[:, :], binv[:, 0:1], lnw[:, :], ALU.mult, ALU.mult))
            link(v.tensor_reduce(sc[:, 1:2], w1, AX.X, ALU.add))
            link(v.tensor_scalar(sc[:, 1:2], sc[:, 1:2], 1.0 / PD, None, ALU.mult))
            link(v.tensor_scalar(w1, w1, sc[:, 1:2], None, ALU.subtract))
            link(v.tensor_tensor(junk, w1, w1, ALU.mult))
            link(v.tensor_reduce(sc[:, 2:3], junk, AX.X, ALU.add))
            link(v.tensor_scalar(sc[:, 2:3], sc[:, 2:3], float(PD), None, ALU.mult))
            v.sem_inc(norm_ready, 1)
            v.wait_ge(set_pool, 2)
            link(v.tensor_reduce(sc[:, 3:4], sc[:, 0:1], AX.X, ALU.max, apply_absolute_value=True))
            link(v.tensor_tensor(sc[:, 3:4], sc[:, 3:4], sc[:, 4:5], ALU.add))
            link(v.tensor_scalar(sc[:, 3:4], sc[:, 3:4], TINY, 1.0 / F16_TOP, ALU.max, ALU.mult))
            link(v.memset(sc[0:2 * QK, 3:4], 1.0))
            link(v.reciprocal(sc[:, 5:6], sc[:, 3:4]))
            link(v.tensor_scalar(w1, w1, sc[:, 5:6], None, ALU.mult))
            link(v.tensor_tensor(sc[:, 6:7], sc[:, 0:1], sc[:, 5:6], ALU.mult))
            link(v.tensor_scalar(diag[:, :], ident[:, :], sc[:, 6:7], None, ALU.mult))
            v.sem_inc(w1_ready, 1)
            v.wait_ge(set_pe, 1)
            link(v.tensor_copy(w_qkv[:, :], ps[0:PD, 0, 0:P]))
            link(v.tensor_copy(bias_qkv[:, :], ps[:, 1, 0:P]))
            link(v.tensor_scalar(p2b[:, :], ones[0:DB, :], fccol[:, 1:2], None, ALU.mult))
            link(v.tensor_reduce(fccol[:, 2:3], fccol[:, 0:1], AX.X, ALU.max, apply_absolute_value=True))
            link(v.tensor_scalar(diag[:, :], ident[:, :], sc[:, 3:4], None, ALU.mult))
            v.sem_inc(tau_ready, 1)
            v.wait_ge(set_pe, 2)
            link(v.tensor_copy(colscale[:, 0:PD], ps[:, 2, 0:PD]))
            link(v.memset(colscale[:, PD:C], 1.0 / SKIP_SCALE))
            for o in range(KT):
                link(v.scalar_tensor_tensor(raw_p[:, o, :], raw_p[:, o, :], binv[:, 1 + o:2 + o], colscale,
                                            ALU.mult, ALU.mult))
            link(v.tensor_reduce(wmax[:, :], raw_p, AX.X, ALU.max, apply_absolute_value=True))
            link(v.tensor_scalar(wp_unscale[:, :], wmax[:, :], TINY, 1.0 / W_TOP, ALU.max, ALU.mult))
            link(v.reciprocal(wmax[:, :], wp_unscale[:, :]))
            for o in range(KT):
                link(v.tensor_scalar(raw_p[:, o, :], raw_p[:, o, :], wmax[:, o:o + 1], None, ALU.mult))
            link(v.tensor_copy(wph0, raw_p))
            link(v.tensor_tensor(wpl0, raw_p, wph0, ALU.subtract))
            link(v.tensor_tensor(shift2[:, :], bn2[:, 2, :], binv[:, 1:4], ALU.mult))
            link(v.tensor_tensor(shift2[:, :], bn2[:, 1, :], shift2[:, :], ALU.subtract))
            link(v.tensor_reduce(fmax[:, :], raw_f, AX.X, ALU.max, apply_absolute_value=True))
            link(v.tensor_scalar(fmax[:, :], fmax[:, :], TINY, 1.0 / F16_TOP, ALU.max, ALU.mult))
            link(v.reciprocal(fsig[:, :], fmax[:, :]))
            link(v.tensor_tensor(raw_f, raw_f, fsig[:, :].unsqueeze(2).to_broadcast([P, JT, DR]), ALU.mult))
            link(v.tensor_copy(fstk[:, :, 0:DR], raw_f))
            link(v.tensor_copy(fstk[:, :, 2 * DR:3 * DR], raw_f))
            link(v.tensor_tensor(fstk[:, :, DR:2 * DR], raw_f, fstk[:, :, 0:DR], ALU.subtract))
            v.sem_inc(wp_ready, 1)
            v.wait_ge(set_pe, 3)
            link(v.tensor_scalar(sc[:, 7:8], ps[:, 3, 0:1], 1.0 / C, None, ALU.mult))
            link(v.tensor_scalar(sc[:, 8:9], ps[:, 3, 1:2], TINY, 1.0 / U_SCALE, ALU.max, ALU.mult))
            link(v.tensor_copy(sc[:, 10:13], ps[:, 3, 2:5]))
            link(v.reciprocal(sc[:, 9:10], sc[:, 8:9]))
            for k in range(KT):
                link(v.tensor_scalar(fold[:, k, :], blk[:, k, :], sc[:, 10 + k:11 + k], sc[:, 7:8],
                                     ALU.mult, ALU.subtract))
            link(v.tensor_scalar(fold[:, :, :], fold[:, :, :], sc[:, 9:10], None, ALU.mult))
            link(v.tensor_scalar(gelu_scale[:, :], fmax[:, :], sc[:, 8:9], None, ALU.mult))
            link(v.tensor_tensor(spread[:, :], ps[:, 4, 0:C], blkt[:, :], ALU.mult))
            v.wait_ge(set_pe, 4)
            link(v.tensor_copy(p1t[:, :, :], ps[:, 5, 0:JT * DR].rearrange("p (j a) -> p j a", j=JT)))
            v.wait_ge(set_pe, 5)
            for k in range(KT):
                src = bank16((6, 7, 0)[k], F16)
                link(v.tensor_copy(wp_hi[:, k, :], src[:, 0:C]))
                link(v.tensor_copy(wp_lo[:, k, :], src[:, 512:512 + C]))
            link(v.tensor_copy(fc1[:, 0:1024], bank16(1, F16)[0:3 * DR, :]))
            link(v.tensor_copy(fc1[:, 1024:DFF], bank16(2, F16)[0:3 * DR, 0:512]))
            v.sem_inc(set_up, 1)

            def statistics(q, s, buf):
                for t in range(TPC):
                    v.wait_ge(tok_taken, q * TPC + t + 1)
                    v.bn_stats(bst[:, s, t, 0, :], xt[:, s, t, 0:C])
                    v.bn_stats(bst[:, s, t, 1, :], xt[:, s, t, 0:PD]).then_inc(a_stat, 1)
                v.sem_inc(x_free[buf], 1)
                v.wait_ge(a_stat, q * (TPC + 2) + TPC)
                v.sem_inc(passed, 1)
                for t in range(TPC):
                    v.bn_aggr(mv[:, s, t, 0, :], bst[:, s, t, 0, :])
                    last = v.bn_aggr(mv[:, s, t, 1, :], bst[:, s, t, 1, :])
                last.then_inc(a_stat, 1)
                v.wait_ge(a_stat, q * (TPC + 2) + TPC + 1)
                v.tensor_scalar(var[:, s, 0, :], mv[:, s, :, 0, 1], LN_IN_EPS, None, ALU.add).then_inc(a_stat, 1)
                v.wait_ge(a_stat, q * (TPC + 2) + TPC + 2)
                v.scalar_tensor_tensor(var[:, s, 1, :], var[:, s, 0, :], LN_ATTN_EPS, mv[:, s, :, 1, 1],
                                       ALU.mult, ALU.add).then_inc(a_var, 1)

            def qkv_parts(q, j, s):
                v.wait_ge(a_rstd, q + 1)
                v.tensor_scalar(skip_s[:, s, :], rstd[:, s, 0, :], SKIP_SCALE, None, ALU.mult).then_inc(a_skip, 1)
                v.wait_ge(a_skip, q * 2 + 1)
                v.scalar_tensor_tensor(skip_b[:, s, :], mv[:, s, :, 0, 0], -1.0, skip_s[:, s, :],
                                       ALU.mult, ALU.mult).then_inc(a_skip, 1)
                v.wait_ge(v_lo, q)
                for t in range(TPC):
                    last = v.scalar_tensor_tensor(qkvf[:, s, t, :], xt[:, s, t, C:C + QKV], rstd[:, s, 1, t:t + 1],
                                                  bias_qkv[:, :], ALU.mult, ALU.add)
                last.then_inc(a_qkv, 1)
                v.wait_ge(a_qkv, q * 4 + 1)
                v.tensor_copy(parts[:, s, :, 0, :], qkvf[:, s, :, 0:2 * QK]).then_inc(a_qkv, 1)
                v.tensor_copy(vs[:, ds(j * TPC, TPC), 0:PD], qkvf[:, s, :, 2 * QK:]).then_inc(v_hi, 1)
                v.wait_ge(a_qkv, q * 4 + 2)
                v.tensor_tensor(rest[:, s, :, :], qkvf[:, s, :, 0:2 * QK], parts[:, s, :, 0, :],
                                ALU.subtract).then_inc(a_qkv, 1)
                v.wait_ge(a_qkv, q * 4 + 3)
                v.tensor_copy(parts[:, s, :, 1, :], rest[:, s, :, :]).then_inc(a_qkv, 1)
                v.wait_ge(a_qkv, q * 4 + 4)
                v.tensor_tensor(parts[:, s, :, 2, :], rest[:, s, :, :], parts[:, s, :, 1, :],
                                ALU.subtract).then_inc(a_parts, 1)
                v.wait_ge(a_parts, q + 1)
                for lo, n in ((0, 3), (3, 2), (5, 1)):
                    v.tensor_copy(stk[:, s, :, lo * QK:(lo + n) * QK].rearrange("p t (l c) -> p t l c", l=n),
                                  parts[:, s, :, 0:n, QK:2 * QK])
                for part, (lo, n) in enumerate(((0, 3), (3, 2), (5, 1))):
                    last = v.tensor_copy(stk[:, s, :, P + lo * QK:P + (lo + n) * QK].rearrange("p t (l c) -> p t l c", l=n),
                                         parts[:, s, :, part:part + 1, 0:QK].to_broadcast([P, TPC, n, QK]))
                last.then_inc(stk_ready, 1)

            def max_tile(gq, idx):
                t, c = divmod(idx, NCH)
                v.wait_ge(mx_ready, gq * (NMX + 1) + idx + 1)
                v.tensor_reduce(mxp[:, t, c:c + 1], ps[:, 4 + idx % 2, :], AX.X, ALU.max).then_inc(mx_free, 1)

            def max_parts(gq):
                v.wait_ge(mx_free, gq * MXC + NMX + 2)
                v.tensor_reduce(nmr[:, :], mxp[:, :, :], AX.X, ALU.max, negate=True).then_inc(nm_step, 1)
                v.wait_ge(nm_step, gq * 6 + 1)
                v.tensor_scalar(nm[:, :], nmr[:, :], EXP_SHIFT, None, ALU.add).then_inc(nm_step, 1)
                v.wait_ge(nm_step, gq * 6 + 2)
                v.tensor_copy(nms[:, :, 0], nm[:, :]).then_inc(nm_step, 1)
                v.wait_ge(nm_step, gq * 6 + 3)
                v.tensor_tensor(nmr[:, :], nm[:, :], nms[:, :, 0], ALU.subtract).then_inc(nm_step, 1)
                v.wait_ge(nm_step, gq * 6 + 4)
                v.tensor_copy(nms[:, :, 1], nmr[:, :]).then_inc(nm_step, 1)
                v.wait_ge(nm_step, gq * 6 + 5)
                v.tensor_tensor(nms[:, :, 2], nmr[:, :], nms[:, :, 1], ALU.subtract).then_inc(nm_step, 1)

            def max_rows(gq, g):
                v.wait_ge(mx_ready, (gq + 1) * (NMX + 1))
                v.tensor_copy(qs[NSTK:NROW, ds(g * CH, CH)], bank16(4, BF16)[0:3, 0:CH]).then_inc(mx_free, 2)

            def high_low(gq, i):
                n = gq * NU + i
                if i in DVE_HIGH:
                    v.wait_ge(exp_done, n + 3)
                    v.wait_ge(pv_done, n + 1)
                    v.tensor_copy(p_hi[:, i % RING, :], p32[:, i % RING, :]).then_inc(high_dve, 1)
                if i in DVE_LOW:
                    if i in DVE_HIGH:
                        v.wait_ge(high_dve, gq * len(DVE_HIGH) + (DVE_HIGH.index(i) + 1))
                    else:
                        v.wait_ge(high_act, gq * len(ACT_HIGH) + (ACT_HIGH.index(i) + 1))
                    v.tensor_tensor(p_lo[:, i % RING, :], p32[:, i % RING, :], p_hi[:, i % RING, :],
                                    ALU.subtract).then_inc(low_dve, 1)

            def take_accumulators(gq):
                v.wait_ge(pv_done, (gq + 1) * NU + RING)
                for h in range(2):
                    v.tensor_copy(acs[:, 2 * h:2 * h + 2, 0:VN],
                                  ps[:, 6 + h, 0:2 * VP].rearrange("p (t n) -> p t n", t=2)[:, :, 0:VN]
                                  ).then_inc(acs_ready, 1)

            def finish_group(gq, g, step):
                at = ds(g * TPC, TPC)
                if step == 0:
                    v.wait_ge(acs_ready, (gq + 1) * 2)
                    v.reciprocal(rsum[:, :], acs[:, :, PD]).then_inc(post, 1)
                    v.tensor_tensor(attn[:, :, :], acs[:, :, 0:PD], acs[:, :, PD + 1:VN], ALU.add).then_inc(post, 1)
                if step == 1:
                    v.wait_ge(post, gq * 5 + 2)
                    v.scalar_tensor_tensor(attn[:, :, :], attn[:, :, :], 0.0,
                                           rsum[:, :].unsqueeze(2).to_broadcast([P, TPC, PD]),
                                           ALU.max, ALU.mult).then_inc(post, 1)
                if step == 2:
                    v.wait_ge(post, gq * 5 + 3)
                    v.tensor_copy(xm_hi[:, at, 0:PD], attn[:, :, :]).then_inc(post, 1)
                if step == 3:
                    v.wait_ge(post, gq * 5 + 4)
                    v.tensor_tensor(xm_lo[:, at, 0:PD], attn[:, :, :], xm_hi[:, at, 0:PD], ALU.subtract).then_inc(post, 1)

            def group(gq, g, first, left):
                for i in range(NU):
                    if i == 0 and not first:
                        take_accumulators(gq - 1)
                    for idx in max_tiles_at(i):
                        if i < MAX_ROWS_AT and left >= 1:
                            max_tile(gq + 1, idx)
                        if i > MAX_ROWS_AT and left >= 2:
                            max_tile(gq + 2, idx)
                    if i == MAX_ROWS_AT - 1 and left >= 1:
                        max_parts(gq + 1)
                    if i + 1 < NU:
                        high_low(gq, i + 1)
                    elif left >= 1:
                        high_low(gq + 1, 0)
                    if i == MAX_ROWS_AT and left >= 1:
                        max_rows(gq + 1, g + 1)
                    if i in FINISH_AT and not first:
                        finish_group(gq - 1, g - 1, FINISH_AT.index(i))

            def copy_turned(q, k):
                v.wait_ge(xt_ready, q * KT + k + 1)
                v.tensor_copy(xc[:, k, :, :].rearrange("p a n -> p (a n)"),
                              bank16(2 + k % 2, F16)).then_inc(xt_copied, 1)

            def residual(q, s, o, stores):
                if o == 0:
                    v.wait_ge(stored[s], stores * 16)
                    v.wait_ge(x_loaded[0], (q + (NA + 1)) * 16)
                v.wait_ge(y_scaled, q * KT + o + 1)
                v.tensor_tensor(x1[:, s, o, :], yb[:, o, :], xin[:, 0, o, :], ALU.add).then_inc(x1_ready, 1)
                if o == KT - 1:
                    v.wait_ge(x1_ready, (q + 1) * KT)
                    v.sem_inc(x_free[0], 1)

            def folded(q, s):
                for t in range(TPC):
                    v.wait_ge(u_ready, q * TPC + t + 1)
                    v.bn_stats(cst[:, s, t, :], ps[:, t % 2, 0:C]).then_inc(c_stat, 1)
                    v.tensor_copy(uraw[:, s, t, :], ps[:, t % 2, C:C + DR]).then_inc(u_taken, 1)
                v.wait_ge(c_stat, q * (TPC + 1) + TPC)
                v.sem_inc(passed, 1)
                for t in range(TPC):
                    last = v.bn_aggr(cmv[:, s, t, :], cst[:, s, t, :])
                last.then_inc(c_stat, 1)
                v.wait_ge(c_stat, q * (TPC + 1) + TPC + 1)
                v.tensor_scalar(cvar[:, s, :], cmv[:, s, :, 1], LN_FFN_EPS, None, ALU.add).then_inc(c_var, 1)

            def split_u(q, s):
                v.wait_ge(c_rstd, q + 1)
                v.wait_ge(u_taken, (q + 1) * TPC)
                v.tensor_tensor(uf[:, s, :, :], uraw[:, s, :, :],
                                crstd[:, s, :].unsqueeze(2).to_broadcast([P, TPC, DR]), ALU.mult).then_inc(u_split, 1)
                v.wait_ge(u_split, q * 4 + 1)
                v.tensor_copy(us[:, s, :, 0:DR], uf[:, s, :, :]).then_inc(u_split, 1)
                v.tensor_copy(us[:, s, :, DR:2 * DR], uf[:, s, :, :]).then_inc(u_split, 1)
                v.wait_ge(u_split, q * 4 + 2)
                v.tensor_tensor(us[:, s, :, 2 * DR:3 * DR], uf[:, s, :, :], us[:, s, :, 0:DR],
                                ALU.subtract).then_inc(u_split, 1)

            def copy_u(q):
                v.wait_ge(ut_ready, q + 1)
                v.tensor_copy(uc[:, :], bank16(3, F16)[0:3 * DR, 0:CH]).then_inc(ut_copied, 1)

            def copy_z(q):
                v.wait_ge(z_ready, q + 1)
                v.tensor_copy(zs[:, :], ps[:, 3, :]).then_inc(z_copied, 1)

            def results(q, s):
                for o in range(KT):
                    v.wait_ge(ff_ready, q * KT + o + 1)
                    v.tensor_tensor(x1[:, s, o, :], ps[:, 5 - o % 2, :], x1[:, s, o, :], ALU.add).then_inc(out_ready, 1)

            def chunk_c(b, j, s, pair, late, with_next):
                q = b * NCH + j
                qa = q + NCH
                folded(q, s)
                if with_next:
                    statistics(qa, s, 1)
                split_u(q, s)
                if late >= 1:
                    residual(q + 1, 1 - s, 0, b * (NCH // 2) + pair + s)
                copy_u(q)
                if with_next:
                    qkv_parts(qa, j, s)
                if late >= 1:
                    residual(q + 1, 1 - s, 1, 0)
                    residual(q + 1, 1 - s, 2, 0)
                copy_z(q)
                if late >= 2:
                    copy_turned(q + 2, 0)
                results(q, s)
                if late >= 2:
                    copy_turned(q + 2, 1)
                    copy_turned(q + 2, 2)

            def phase_c(b, with_next):
                q0 = b * NCH
                for k in range(KT):
                    copy_turned(q0, k)
                for o in range(KT):
                    residual(q0, 0, o, b * (NCH // 2))
                for k in range(KT):
                    copy_turned(q0 + 1, k)
                with v.Fori(0, NCH // 2 - 1) as jj:
                    for s in range(2):
                        chunk_c(b, jj * 2 + s, s, jj, 2, with_next)
                chunk_c(b, NCH - 2, 0, NCH // 2 - 1, 1, with_next)
                chunk_c(b, NCH - 1, 1, NCH // 2 - 1, 0, with_next)

            def phase_b(b):
                gq0 = b * NCH
                for idx in range(NMX):
                    max_tile(gq0, idx)
                max_parts(gq0)
                max_rows(gq0, 0)
                for idx in range(MAX_EARLY):
                    max_tile(gq0 + 1, idx)
                high_low(gq0, 0)
                group(gq0, 0, True, 2)
                with v.Fori(1, NCH - 2) as g:
                    group(b * NCH + g, g, False, 2)
                group(gq0 + (NCH - 2), NCH - 2, False, 1)
                group(gq0 + (NCH - 1), NCH - 1, False, 0)
                take_accumulators(gq0 + (NCH - 1))
                for step in range(len(FINISH_AT)):
                    finish_group(gq0 + (NCH - 1), NCH - 1, step)

            with v.Fori(0, NA) as jj:
                for s in range(2):
                    statistics(jj * 2 + s, s, s)
                    qkv_parts(jj * 2 + s, jj * 2 + s, s)
            with v.Fori(0, B - 1) as b:
                phase_b(b)
                phase_c(b, True)
            phase_b(B - 1)
            phase_c(B - 1, False)

        @block.gpsimd
        def _(g):
            g.sem_inc(low_pool, len(POOL_LOW))
            g.sem_inc(skip_lo, 1)
            g.sem_inc(v_lo, 1)
            g.wait_ge(bn_var_ready, 1)
            g.tensor_tensor(binv[:, :], bvar[:, :], expo[:, 0:4], ALU.pow).then_inc(set_pool, 1)
            g.wait_ge(norm_ready, 1)
            g.tensor_tensor(sc[:, 4:5], sc[:, 2:3], half[:, :], ALU.pow).then_inc(set_pool, 1)

            def rstd_a(q, s):
                g.wait_ge(a_var, q + 1)
                g.tensor_tensor(rstd[:, s, :, :].rearrange("p a t -> p (a t)"),
                                var[:, s, :, :].rearrange("p a t -> p (a t)"), expo[:, :], ALU.pow).then_inc(a_rstd, 1)

            def low_a(q, j, s):
                tiles = ds(j * TPC, TPC)
                g.wait_ge(v_hi, q + 1)
                g.tensor_tensor(vs[:, tiles, PD + 1:VN], qkvf[:, s, :, 2 * QK:], vs[:, tiles, 0:PD],
                                ALU.subtract).then_inc(v_lo, 1)
                g.wait_ge(skip_hi, q + 1)
                g.tensor_tensor(xm_lo[:, tiles, PD:C], xt[:, s, :, PD:C], xm_hi[:, tiles, PD:C],
                                ALU.subtract).then_inc(skip_lo, 1)

            def low_parts(gq):
                for i in POOL_LOW:
                    if i in DVE_HIGH:
                        g.wait_ge(high_dve, gq * len(DVE_HIGH) + (DVE_HIGH.index(i) + 1))
                    else:
                        g.wait_ge(high_act, gq * len(ACT_HIGH) + (ACT_HIGH.index(i) + 1))
                    g.tensor_tensor(p_lo[:, i % RING, :], p32[:, i % RING, :], p_hi[:, i % RING, :],
                                    ALU.subtract).then_inc(low_pool, 1)

            def chunk_c(b, j, s, with_next):
                q = b * NCH + j
                g.wait_ge(c_var, q + 1)
                g.tensor_tensor(crstd[:, s, :], cvar[:, s, :], expo[:, 0:TPC], ALU.pow).then_inc(c_rstd, 1)
                if with_next:
                    rstd_a(q + NCH, s)
                    low_a(q + NCH, j, s)

            def phases_bc(b, with_next):
                with g.Fori(0, NCH) as gr:
                    low_parts(b * NCH + gr)
                with g.Fori(0, NCH // 2) as jj:
                    for s in range(2):
                        chunk_c(b, jj * 2 + s, s, with_next)

            with g.Fori(0, NA) as jj:
                for s in range(2):
                    rstd_a(jj * 2 + s, s)
                    low_a(jj * 2 + s, jj * 2 + s, s)
            with g.Fori(0, B - 1) as b:
                phases_bc(b, True)
            phases_bc(B - 1, False)


_INS = {"x": "x", "L0_conv_ln_w": "ln_w", "L0_conv_ln_b": "ln_b", "L0_conv_w_qkv": "w_qkv",
        "L0_conv_bn1_g": "bn1_g", "L0_conv_bn1_b": "bn1_b", "L0_conv_bn1_m": "bn1_m", "L0_conv_bn1_v": "bn1_v",
        "L0_conv_w_proj": "w_proj", "L0_conv_bn2_g": "bn2_g", "L0_conv_bn2_b": "bn2_b", "L0_conv_bn2_m": "bn2_m",
        "L0_conv_bn2_v": "bn2_v", "L0_ffn_c_fc_1": "c_fc_1", "L0_ffn_c_fc_2": "c_fc_2",
        "L0_ffn_c_proj_1": "c_proj_1", "L0_ffn_c_proj_2": "c_proj_2"}


def shape_constants():
    ch = np.arange(C)
    blk = (ch[:, None] // DB == np.arange(DR)[None, :]).astype(np.float32)
    return {
        "ident": np.eye(P, dtype=np.float32),
        "rep": (ch[None, :] % DB == np.arange(DB)[:, None]).astype(np.float32),
        "blk": blk,
        "blkt": np.ascontiguousarray(np.concatenate([blk.T] * 4, axis=0)),
    }


def kernel(**inputs):
    import concourse.bacc as bacc
    from concourse.bass_utils import run_bass_kernel_spmd

    nc = bacc.Bacc("TRN2", target_bir_lowering=False, num_devices=1)
    arrays, aps = {}, {}
    for name, short in _INS.items():
        arrays[f"in_{short}"] = np.ascontiguousarray(inputs[name])
    for short, a in shape_constants().items():
        arrays[f"in_{short}"] = a
    for key, a in arrays.items():
        aps[key[3:]] = nc.dram_tensor(key, a.shape, mybir.dt.from_np(a.dtype), kind="ExternalInput").ap()
    aps["out"] = nc.dram_tensor("out_0", (B, C, H, W), F32, kind="ExternalOutput").ap()
    build(nc, aps)
    r = run_bass_kernel_spmd(nc, [arrays], core_ids=[0])
    return r.results[0]["out_0"]
```

```python
from contextlib import ExitStack

import numpy as np
import concourse.bass as bass
from concourse import mybir

F32, F16, BF16 = mybir.dt.float32, mybir.dt.float16, mybir.dt.bfloat16
ALU = mybir.AluOpType
ACT = mybir.ActivationFunctionType
AX = mybir.AxisListType
ds = bass.ds

B, C, H, W = 4, 384, 64, 64
N = H * W
P = 128
PD, QK = 96, 16
QKV = 2 * QK + PD
KT = C // P
CH = 512
NCH = N // CH
TPC = CH // P
NA = NCH // 2
NT = N // P
DFF, DR, DB = 1536, 32, 12
JT = DFF // P
NSTK = 6 * QK
NROW = NSTK + 3
VP = 2 * PD + 2
VN = 2 * PD + 1
KPU = 2
NU = NT // KPU
UW = KPU * CH
RING = 4

LN_IN_EPS, LN_ATTN_EPS, LN_FFN_EPS, BN_EPS = 1e-6, 1e-5, 1e-5, 1e-5
F16_TOP = 2.0 ** 14
SKIP_SCALE = 2.0 ** 9
U_SCALE = 2.0 ** 9
W_TOP = 2.0 ** 12
TINY = 1e-30
SCALE = QK ** -0.5
EXP_SHIFT = 10 / SCALE

POOL_LOW = tuple(i for i in range(NU) if i not in (2, 7, 12))
DVE_HIGH = (2, 7)
DVE_LOW = tuple(i for i in range(NU) if i not in POOL_LOW)
ACT_HIGH = tuple(i for i in range(NU) if i not in DVE_HIGH)
NMX = TPC * NCH
LEAD = 3
MAX_AT = [2, 1, 3, 2, 2, 2, 1, 3, 3, 2, 1, 0, 3, 3, 2, 2]
MAX_ROWS_AT = 11
FINISH_AT = (3, 5, 13, 14)
MAX_EARLY = sum(MAX_AT[MAX_ROWS_AT:])
assert sum(MAX_AT) == NMX
N_LOADS = 20
PRODUCTS_AHEAD, PRODUCTS_AT = 7, [2, 2, 2, 2, 2, 2, 2, 2, 2, 2, 0, 0]
assert PRODUCTS_AHEAD + sum(PRODUCTS_AT) == 3 * KT * KT
EARLY_TURNS = {0: (0, 0, 5), 1: (0, 1, 4), 2: (0, 2, 5), 12: (1, 0, 5), 14: (1, 1, 4), 15: (1, 2, 5)}
EARLY_PRODUCTS, PRODUCTS_FROM = 3, 3
EARLY_OUT = (8, 11, 14)
EARLY_COPIES = {1: (0, 0, 5), 2: (0, 1, 4), 3: (0, 2, 5), 13: (1, 0, 5), 15: (1, 1, 4)}
OUT_AT = (2, 6, 10)
MXC = NMX + 2


TILE_BANKS = (0, 1, 6, 7)
XT_BANKS = (2, 6, 2)
STK_BANK = 7
EXPAND_BANKS = (5, 4, 2)


FIRST_MAX_AT = (2, 4, 7, 9)
FIRST_MAX_BANK = 2


def max_tiles_at(i):
    first = sum(MAX_AT[MAX_ROWS_AT:i]) if i >= MAX_ROWS_AT else MAX_EARLY + sum(MAX_AT[:i])
    return range(first, first + MAX_AT[i])


def build(nc, A):
    ctx = ExitStack()
    with ctx:
        def sb(name, shape, dt=F32):
            return ctx.enter_context(nc.sbuf_tensor(name, shape, dt))

        def sem(name):
            return ctx.enter_context(nc.semaphore(name))

        ident = sb("ident", [P, P])
        ident_h = sb("ident_h", [P, P], F16)
        ident_b = sb("ident_b", [P, P], BF16)
        ones = sb("ones", [P, P])
        expo = sb("expo", [P, 8])
        table = sb("table", [P, 1])
        half = sb("half", [P, 1])
        w_qkv = sb("w_qkv", [PD, QKV])
        bias_qkv = sb("bias_qkv", [P, QKV])
        wp_hi = sb("wp_hi", [P, KT, C], F16)
        wp_lo = sb("wp_lo", [P, KT, C], F16)
        wp_unscale = sb("wp_unscale", [P, KT])
        shift2 = sb("shift2", [P, KT])
        fold = sb("fold", [P, KT, DR])
        fc1 = sb("fc1", [3 * DR, DFF], F16)
        gelu_scale = sb("gelu_scale", [P, JT])
        p1t = sb("p1t", [P, JT, DR])
        spread = sb("spread", [P, C])
        ks = sb("ks", [P, N], BF16)
        qs = sb("qs", [P, N], BF16)
        vs = sb("vs", [P, NT, VP], F16)
        xm_hi = sb("xm_hi", [P, NT, C], F16)
        xm_lo = sb("xm_lo", [P, NT, C], F16)
        xin = sb("xin", [P, 2, KT, CH])
        pool32 = sb("pool32", [P, 8192])
        p32 = pool32[:, 0:RING * UW].rearrange("p (r n) -> p r n", r=RING)
        p_hi = pool32[:, 4096:6144].bitcast(F16).rearrange("p (r n) -> p r n", r=RING)
        p_lo = pool32[:, 6144:8192].bitcast(F16).rearrange("p (r n) -> p r n", r=RING)
        gel = pool32[:, 0:JT * CH].rearrange("p (j n) -> p j n", j=JT)
        xt = sb("xt", [P, 2, TPC, C + QKV])
        qkvf = sb("qkvf", [P, 2, TPC, QKV])
        rest = sb("rest", [P, 2, TPC, 2 * QK])
        parts = sb("parts", [P, 2, TPC, 3, 2 * QK], BF16)
        stk = sb("stk", [P, 2, TPC, 2 * P], BF16)
        bst = sb("bst", [P, 2, TPC, 2, 6])
        mv = sb("mv", [P, 2, TPC, 2, 2])
        var = sb("var", [P, 2, 2, TPC])
        rstd = sb("rstd", [P, 2, 2, TPC])
        skip_s = sb("skip_s", [P, 2, TPC])
        skip_b = sb("skip_b", [P, 2, TPC])
        mxp = sb("mxp", [P, TPC, NCH])
        nm = sb("nm", [P, TPC])
        nmr = sb("nmr", [P, TPC])
        nms = sb("nms", [P, TPC, 3], BF16)
        acs = sb("acs", [P, TPC, VP])
        attn = sb("attn", [P, TPC, PD])
        rsum = sb("rsum", [P, TPC])
        xc = sb("xc", [P, KT, 2, CH], F16)
        yb = sb("yb", [P, KT, CH])
        x1 = sb("x1", [P, 2, KT, CH])
        cst = sb("cst", [P, 2, TPC, 6])
        cmv = sb("cmv", [P, 2, TPC, 2])
        cvar = sb("cvar", [P, 2, TPC])
        crstd = sb("crstd", [P, 2, TPC])
        uraw = sb("uraw", [P, P])
        uf = sb("uf", [P, 2, TPC, DR])
        us = sb("us", [P, 2, TPC, 3 * DR], F16)
        uc = sb("uc", [3 * DR, CH], F16)
        zs = sb("zs", [P, CH])
        raw_qkv = sb("raw_qkv", [P, PD])
        lnw = sb("lnw", [P, PD])
        lnb = sb("lnb", [P, PD])
        bn1 = sb("bn1", [P, 4])
        bn2 = sb("bn2", [P, 4, KT])
        bvar = sb("bvar", [P, 4])
        binv = sb("binv", [P, 4])
        sc = sb("sc", [P, 16])
        diag = sb("diag", [P, P])
        fccol = sb("fccol", [DB, 4])
        rep = sb("rep", [DB, C])
        p2b = sb("p2b", [DB, P])
        blk = sb("blk", [P, KT, DR])
        blkt = sb("blkt", [P, C])
        fmax = sb("fmax", [P, JT])
        fsig = sb("fsig", [P, JT])
        wmax = sb("wmax", [P, KT])
        raw_p = pool32[:, 0:1152].rearrange("p (t n) -> p t n", t=KT)
        wph0 = pool32[:, 1152:1728].bitcast(F16).rearrange("p (t n) -> p t n", t=KT)
        wpl0 = pool32[:, 1728:2304].bitcast(F16).rearrange("p (t n) -> p t n", t=KT)
        colscale = pool32[:, 2304:2688]
        raw_f = pool32[:, 2688:3072].rearrange("p (j n) -> p j n", j=JT)
        fstk = pool32[:, 3072:3648].bitcast(F16).rearrange("p (j n) -> p j n", j=JT)
        raw_p1 = pool32[0:DR, 3648:5184]
        w1 = pool32[:, 5184:5280]
        junk = pool32[:, 5280:5376]

        ps = ctx.enter_context(nc.psum_tensor("ps", [P, 8, 512], F32))

        def bank16(b, dt):
            return ps[:, b, :].bitcast(dt)

        w_loaded = sem("w_loaded")
        set_dve = sem("set_dve")
        set_pe = sem("set_pe")
        set_pool = sem("set_pool")
        bn_var_ready = sem("bn_var_ready")
        norm_ready = sem("norm_ready")
        w1_ready = sem("w1_ready")
        tau_ready = sem("tau_ready")
        wp_ready = sem("wp_ready")
        set_up = sem("set_up")
        x_loaded = [sem("x_loaded0"), sem("x_loaded1")]
        x_free = [sem("x_free0"), sem("x_free1")]
        tok_ready = sem("tok_ready")
        tok_taken = sem("tok_taken")
        a_stat = sem("a_stat")
        a_var = sem("a_var")
        a_rstd = sem("a_rstd")
        a_skip = sem("a_skip")
        a_parts = sem("a_parts")
        a_qkv = sem("a_qkv")
        stk_ready = sem("stk_ready")
        stk_turned = sem("stk_turned")
        stk_copied = sem("stk_copied")
        skip_f = sem("skip_f")
        skip_hi = sem("skip_hi")
        skip_lo = sem("skip_lo")
        v_hi = sem("v_hi")
        v_lo = sem("v_lo")
        st_ready = sem("st_ready")
        exp_done = sem("exp_done")
        high_act = sem("high_act")
        high_dve = sem("high_dve")
        low_dve = sem("low_dve")
        low_pool = sem("low_pool")
        pv_done = sem("pv_done")
        mx_ready = sem("mx_ready")
        mx_free = sem("mx_free")
        nm_step = sem("nm_step")
        acs_ready = sem("acs_ready")
        passed = sem("passed")
        post = sem("post")
        xt_ready = sem("xt_ready")
        xt_copied = sem("xt_copied")
        y_ready = sem("y_ready")
        y_scaled = sem("y_scaled")
        x1_ready = sem("x1_ready")
        u_ready = sem("u_ready")
        u_taken = sem("u_taken")
        u_turned = sem("u_turned")
        x1t_ready = sem("x1t_ready")
        c_stat = sem("c_stat")
        c_var = sem("c_var")
        c_rstd = sem("c_rstd")
        u_split = sem("u_split")
        ut_ready = sem("ut_ready")
        ut_copied = sem("ut_copied")
        h_ready = sem("h_ready")
        g_ready = sem("g_ready")
        z_ready = sem("z_ready")
        z_copied = sem("z_copied")
        ff_ready = sem("ff_ready")
        out_ready = sem("out_ready")
        stored = [sem("stored0"), sem("stored1")]

        x_v = A["x"].rearrange("b (k p) h w -> p b k (h w)", p=P)
        out_v = A["out"].rearrange("b (k p) h w -> p b k (h w)", p=P)

        block = ctx.enter_context(nc.Block())

        @block.sync
        def _(sp):
            def col(v):
                return v.rearrange("(p o) -> p o", o=1)

            loads = [
                (ident[:, :], A["ident"]), (rep[:, :], A["rep"]),
                (blk[:, :, :], A["blk"].rearrange("(k p) a -> p k a", p=P)), (blkt[:, :], A["blkt"]),
                (raw_qkv[:, :], A["w_qkv"]),
                (lnw[:, :], A["ln_w"].partition_broadcast(P)), (lnb[:, :], A["ln_b"].partition_broadcast(P)),
                (bn1[:, 0:1], col(A["bn1_g"])), (bn1[:, 1:2], col(A["bn1_b"])),
                (bn1[:, 2:3], col(A["bn1_m"])), (bn1[:, 3:4], col(A["bn1_v"])),
                (bn2[:, 0, :], A["bn2_g"].rearrange("(k p) -> p k", p=P)),
                (bn2[:, 1, :], A["bn2_b"].rearrange("(k p) -> p k", p=P)),
                (bn2[:, 2, :], A["bn2_m"].rearrange("(k p) -> p k", p=P)),
                (bn2[:, 3, :], A["bn2_v"].rearrange("(k p) -> p k", p=P)),
                (raw_p, A["w_proj"].rearrange("(k p) c -> p k c", p=P)),
                (raw_f, A["c_fc_1"].rearrange("(j p) a -> p j a", p=P)),
                (raw_p1, A["c_proj_1"]),
                (fccol[:, 0:1], A["c_fc_2"].rearrange("a b -> b a")), (fccol[:, 1:2], A["c_proj_2"]),
            ]
            assert len(loads) == N_LOADS
            with nc.allow_non_contiguous_dma(reason="small vectors, once"):
                for dst, src in loads:
                    sp.dma_start(dst, src).then_inc(w_loaded, 16)

            def load_x(b, j, s, n):
                sp.wait_ge(x_free[s], n + 1)
                src = x_v[:, ds(b, 1), :, ds(j * CH, CH)].rearrange("p o k n -> p (o k) n")
                sp.dma_start(xin[:, s, :, :], src).then_inc(x_loaded[s], 16)

            def store(b, j, s):
                sp.wait_ge(out_ready, (b * NCH + j + 1) * KT)
                dst = out_v[:, ds(b, 1), :, ds(j * CH, CH)].rearrange("p o k n -> p (o k) n")
                sp.dma_start(dst, x1[:, s, :, :]).then_inc(stored[s], 16)

            def phase_c(b, with_next):
                load_x(b, 0, 0, b * NCH + NA)
                if with_next:
                    load_x(b + 1, 0, 1, b * NCH + NA)
                load_x(b, 1, 0, b * NCH + (NA + 1))

                def chunk(j, s, late):
                    if with_next and late > 0:
                        load_x(b + 1, j + 1, 1, b * NCH + (NA + 1) + j)
                    if late > 1:
                        load_x(b, j + 2, 0, b * NCH + (NA + 2) + j)
                    store(b, j, s)

                with sp.Fori(0, NCH // 2 - 1) as jj:
                    for s in range(2):
                        chunk(jj * 2 + s, s, 2)
                chunk(NCH - 2, 0, 1)
                chunk(NCH - 1, 1, 0)

            with sp.Fori(0, NA) as jj:
                for s in range(2):
                    load_x(0, jj * 2 + s, s, jj)
            with sp.Fori(0, B - 1) as b:
                phase_c(b, True)
            phase_c(B - 1, False)
            for s in range(2):
                sp.wait_ge(stored[s], 16 * B * NCH // 2)

        @block.tensor
        def _(pe):
            mm = pe.matmul

            pe.wait_ge(w1_ready, 1)
            pe.transpose(ps[0:PD, 0, 0:P], w1, ident[:, :])
            mm(ps[:, 1, 0:P], ones[:, :], diag[:, :], start=True, stop=True).then_inc(set_pe, 1)
            pe.wait_ge(tau_ready, 1)
            mm(ps[:, 2, 0:PD], ones[:, :], diag[:, 2 * QK:], start=True, stop=True).then_inc(set_pe, 1)
            mm(ps[:, 3, 0:1], ones[0:DB, :], fccol[:, 0:1], start=True, stop=True)
            mm(ps[:, 3, 1:2], ones[0:DB, :], fccol[:, 2:3], start=True, stop=True)
            for k in range(KT):
                mm(ps[:, 3, 2 + k:3 + k], rep[:, k * P:(k + 1) * P], fccol[:, 0:1], start=True, stop=True)
            mm(ps[:, 4, 0:C], p2b[:, :], rep[:, :], start=True, stop=True).then_inc(set_pe, 1)
            for j in range(JT):
                last = pe.transpose(ps[:, 5, j * DR:(j + 1) * DR], raw_p1[:, j * P:(j + 1) * P], ident[0:DR, 0:DR])
            last.then_inc(set_pe, 1)
            pe.wait_ge(wp_ready, 1)
            for k in range(KT):
                for part, src in ((0, wph0), (1, wpl0)):
                    for o in range(KT):
                        last = pe.transpose(bank16((6, 7, 0)[k], F16)[:, part * 512 + o * P:part * 512 + (o + 1) * P],
                                            src[:, o, k * P:(k + 1) * P], ident_h[:, :])
            for j in range(JT):
                last = pe.transpose(bank16(1 + j // 8, F16)[0:3 * DR, (j % 8) * P:(j % 8 + 1) * P],
                                    fstk[:, j, :], ident_h[:, :])
            last.then_inc(set_pe, 1)
            pe.wait_ge(set_up, 2)

            def tokens(qa, buf, tiles, loads, after_u=None):
                for t in tiles:
                    if t == 0:
                        pe.wait_ge(x_loaded[buf], loads * 16)
                        pe.wait_ge(tok_taken, qa * TPC)
                    if after_u is not None:
                        pe.wait_ge(c_stat, after_u * (TPC + 1) + t + 1)
                    bk = ps[:, TILE_BANKS[t], :]
                    for k in range(KT):
                        pe.transpose(bk[:, k * P:(k + 1) * P], xin[:, buf, k, t * P:(t + 1) * P], ident[:, :])
                    mm(bk[:, C:C + QKV], xin[0:PD, buf, 0, t * P:(t + 1) * P], w_qkv[:, :],
                       start=True, stop=True).then_inc(tok_ready, 1)

            def turn_stacks(qa, s, bank):
                pe.wait_ge(stk_ready, qa + 1)
                pe.wait_ge(stk_copied, qa)
                pe.wait_ge(tok_taken, (qa + 1) * TPC)
                bk = bank16(bank, BF16)
                for t in range(TPC):
                    pe.transpose(bk[0:NROW, t * P:(t + 1) * P], stk[:, s, t, 0:NROW], ident_b[:, :])
                    last = pe.transpose(bk[0:NSTK, CH + t * P:CH + (t + 1) * P], stk[:, s, t, P:P + NSTK], ident_b[:, :])
                last.then_inc(stk_turned, 1)

            def max_tile(gq, g, idx):
                t, c = divmod(idx, NCH)
                pe.wait_ge(mx_free, gq * MXC + idx + 1)
                mm(ps[:, 4 + idx % 2, :], qs[0:NSTK, ds(g * CH + t * P, P)], ks[0:NSTK, c * CH:(c + 1) * CH],
                   start=True, stop=True).then_inc(mx_ready, 1)

            def first_max_tile(before, keys, t, bank, credits):
                pe.wait_ge(mx_free, before + t + credits)
                mm(ps[:, bank, :], qs[0:NSTK, t * P:(t + 1) * P], ks[0:NSTK, keys], start=True, stop=True
                   ).then_inc(mx_ready, 1)

            def first_max_chunk(gq, c, copied):
                pe.wait_ge(stk_copied, copied)
                for t in range(TPC):
                    first_max_tile(gq * MXC + c * TPC, ds(c * CH, CH), t, 4 + t % 2, 1)

            def max_rows(gq):
                pe.wait_ge(mx_free, gq * MXC + NMX + 1)
                pe.wait_ge(nm_step, (gq + 1) * 6)
                for t in range(TPC):
                    last = pe.transpose(bank16(4, BF16)[0:3, t * P:(t + 1) * P], nms[:, t, :], ident_b[:, :])
                last.then_inc(mx_ready, 1)

            def scores(gq, g, i):
                n = gq * NU + i
                if i == 0:
                    pe.wait_ge(mx_free, (gq + 1) * MXC + 2)
                pe.wait_ge(exp_done, n + 1)
                for h in range(KPU):
                    kt = KPU * i + h
                    last = mm(ps[:, 2 * (i % 2) + h, :], ks[0:NROW, kt * P:(kt + 1) * P], qs[0:NROW, ds(g * CH, CH)],
                              start=True, stop=True)
                last.then_inc(st_ready, 1)

            def values(gq, i, between=None):
                if i in POOL_LOW:
                    pe.wait_ge(low_pool, (gq + 1) * len(POOL_LOW) + (POOL_LOW.index(i) + 1))
                else:
                    pe.wait_ge(low_dve, (gq + 1) * len(DVE_LOW) + (DVE_LOW.index(i) + 1))
                if i == 0:
                    pe.wait_ge(acs_ready, gq * 2 + 0)
                for h in range(KPU):
                    if h == 1 and between:
                        between()
                    kt = KPU * i + h
                    for t in range(TPC):
                        acc = ps[:, 6 + t // 2, (t % 2) * VP:(t % 2) * VP + VN]
                        at = h * CH + t * P
                        mm(acc, p_hi[:, i % RING, at:at + P], vs[:, kt, 0:VN],
                           start=(kt == 0 and t % 2 == 0), stop=False, skip_group_check=True)
                        last = mm(acc[:, 0:PD + 1], p_lo[:, i % RING, at:at + P], vs[:, kt, 0:PD + 1],
                                  start=False, stop=(kt == NT - 1), skip_group_check=True)
                last.then_inc(pv_done, 1)

            def turn_early(q0, i):
                j, k, bank = EARLY_TURNS[i]
                if j == 1:
                    pe.wait_ge(y_scaled, q0 * KT + (3 if bank == 4 else 2))
                turn_input(j, q0 + j, k, bank)

            def group(gq, g, left):
                q0 = gq - (NCH - 1)
                products = project_all(q0, q0)
                for i in range(NU):
                    tiles = list(max_tiles_at(i))
                    if left == 0 and i in EARLY_TURNS:
                        turn_early(q0, i)

                    def next_max():
                        if tiles and i < MAX_ROWS_AT and left >= 1:
                            max_tile(gq + 1, g + 1, tiles.pop(0))
                        if tiles and i > MAX_ROWS_AT and left >= 2:
                            max_tile(gq + 2, g + 2, tiles.pop(0))

                    next_max()
                    if i + LEAD < NU:
                        scores(gq, g, i + LEAD)
                    elif left >= 1:
                        scores(gq + 1, g + 1, i + LEAD - NU)
                    next_max()
                    values(gq, i, next_max)
                    if left == 0 and i >= PRODUCTS_FROM:
                        for _ in range(EARLY_PRODUCTS):
                            next(products, None)
                    if i == MAX_ROWS_AT and left >= 1:
                        max_rows(gq + 1)

            def turn_input(j, q, k, bank):
                if k == 0:
                    pe.wait_ge(post, (q + 1) * 5)
                    pe.wait_ge(skip_lo, q + 2)
                if k == 2:
                    pe.wait_ge(xt_copied, q * KT + 1)
                bk = bank16(bank, F16)
                for part, src in ((0, xm_hi), (1, xm_lo)):
                    for t in range(TPC):
                        last = pe.transpose(bk[:, part * CH + t * P:part * CH + (t + 1) * P],
                                            src[:, ds(j * TPC + t, 1), k * P:(k + 1) * P].rearrange("p o n -> p (o n)"),
                                            ident_h[:, :])
                last.then_inc(xt_ready, 1)

            def project(q, o, outs):
                bk = ps[:, 4 + o % 2, :]
                terms = [(w, k, part) for k in range(KT) for w, part in ((wp_hi, 0), (wp_lo, 0), (wp_hi, 1))]
                for n, (w, k, part) in enumerate(terms):
                    if n == 0:
                        pe.wait_ge(xt_copied, (q + 1) * KT)
                        if o == 2:
                            pe.wait_ge(y_scaled, q * KT + 1)
                        else:
                            pe.wait_ge(out_ready, outs * KT)
                    last = mm(bk, w[:, k, o * P:(o + 1) * P], xc[:, k, part, :], start=(n == 0), stop=(n == len(terms) - 1))
                    if n == len(terms) - 1:
                        last.then_inc(y_ready, 1)
                    yield

            def fold_u(q, s, turned, stacks):
                pe.wait_ge(x1_ready, (q + 1) * KT)
                pe.wait_ge(z_copied, q)
                for k in range(KT):
                    for c in range(TPC):
                        last = mm(ps[c * DR:(c + 1) * DR, 3, 0:P], fold[:, k, :], x1[:, s, k, c * P:(c + 1) * P],
                                  start=(k == 0), stop=(k == KT - 1), tile_position=(0, c * DR))
                last.then_inc(u_ready, 1)
                pe.wait_ge(g_ready, q * JT + len(TILE_BANKS))
                for t in range(TPC):
                    if TILE_BANKS[t] == XT_BANKS[1]:
                        pe.wait_ge(xt_copied, turned)
                    if TILE_BANKS[t] == STK_BANK:
                        pe.wait_ge(stk_copied, stacks)
                    for k in range(KT):
                        last = pe.transpose(ps[:, TILE_BANKS[t], k * P:(k + 1) * P], x1[:, s, k, t * P:(t + 1) * P],
                                            ident[:, :])
                    last.then_inc(x1t_ready, 1)
                pe.wait_ge(u_taken, q + 1)
                pe.transpose(ps[:, 3, 0:P], uraw[:, :], ident[:, :]).then_inc(u_turned, 1)

            def turn_u(q, s):
                pe.wait_ge(u_split, (q + 1) * 4)
                for t in range(TPC):
                    last = pe.transpose(bank16(3, F16)[0:3 * DR, t * P:(t + 1) * P], us[:, s, t, :], ident_h[:, :])
                last.then_inc(ut_ready, 1)

            def up(q, j):
                if j == 0:
                    pe.wait_ge(ut_copied, q + 1)
                pe.wait_ge(g_ready, q * JT + j + 1)
                mm(ps[:, TILE_BANKS[j % 4], :], fc1[:, j * P:(j + 1) * P], uc[:, :], start=True, stop=True).then_inc(h_ready, 1)

            def down(q, r):
                pe.wait_ge(g_ready, q * JT + 4 * r + 4 + len(TILE_BANKS))
                for c in range(4):
                    last = mm(ps[c * DR:(c + 1) * DR, 3, :], p1t[:, 4 * r + c, :], gel[:, 4 * r + c, :],
                              start=(r == 0), stop=(r == JT // 4 - 1), tile_position=(0, c * DR))
                if r == JT // 4 - 1:
                    last.then_inc(z_ready, 1)

            def expand(q, done):
                pe.wait_ge(z_copied, q + 1)
                pe.wait_ge(y_scaled, done[0] * KT)
                for o in range(KT):
                    if o == KT - 1:
                        pe.wait_ge(xt_copied, done[1] * KT)
                    mm(ps[:, EXPAND_BANKS[o], :], spread[:, o * P:(o + 1) * P], zs[:, :], start=True, stop=True).then_inc(ff_ready, 1)

            def chunk_c(b, j, s, late, with_next, next_max=True):
                q = b * NCH + j
                qa = q + NCH
                loads = b * NCH + j + (NA + 1)
                if with_next:
                    tokens(qa, 1, range(2), loads, after_u=q)
                turn_u(q, s)
                if with_next:
                    tokens(qa, 1, range(2, TPC), loads, after_u=q)
                products = project_all(q + 1, q) if late >= 1 else iter(())
                for _ in range(PRODUCTS_AHEAD):
                    next(products, None)
                for n in range(JT):
                    if with_next and n < TPC:
                        pe.wait_ge(tok_taken, qa * TPC + n + 1)
                    up(q, n)
                    if with_next and next_max and n in FIRST_MAX_AT:
                        if n == FIRST_MAX_AT[0]:
                            pe.wait_ge(stk_copied, qa)
                            pe.wait_ge(out_ready, q * KT)
                        first_max_tile((b + 1) * NCH * MXC + (j - 1) * TPC, ds((j - 1) * CH, CH),
                                       FIRST_MAX_AT.index(n), FIRST_MAX_BANK, 2)
                    for _ in range(PRODUCTS_AT[n]):
                        next(products, None)
                    if n == 6:
                        down(q, 0)
                    if n == 10:
                        down(q, 1)
                for _ in products:
                    pass
                if late >= 2:
                    pe.wait_ge(out_ready, q * KT)
                    if with_next and next_max:
                        pe.wait_ge(mx_free, (b + 1) * NCH * MXC + j * TPC + 2)
                    turn_input(j + 2, q + 2, 0, XT_BANKS[0])
                down(q, 2)
                if with_next:
                    turn_stacks(qa, s, STK_BANK)
                if late >= 2:
                    turn_input(j + 2, q + 2, 1, XT_BANKS[1])
                    turn_input(j + 2, q + 2, 2, XT_BANKS[2])
                if late >= 1:
                    fold_u(q + 1, 1 - s, (q + 2) * KT + 2 if late == 2 else (q + 2) * KT,
                           qa + 1 if with_next else B * NCH)
                expand(q, (q + min(late, 1) + 1, q + late + 1))

            def project_all(q, outs):
                for o in range(KT):
                    yield from project(q, o, outs)

            def phase_c(b, with_next):
                q0 = b * NCH
                pe.wait_ge(acs_ready, (q0 + NCH) * 2)
                fold_u(q0, 0, (q0 + 1) * KT, q0 + NCH if with_next else B * NCH)
                for s in range(2):
                    chunk_c(b, s, s, 2, with_next, next_max=s > 0)
                with pe.Fori(1, NCH // 2 - 1) as jj:
                    for s in range(2):
                        chunk_c(b, jj * 2 + s, s, 2, with_next)
                chunk_c(b, NCH - 2, 0, 1, with_next)
                chunk_c(b, NCH - 1, 1, 0, with_next)

            def phase_b(b):
                gq0 = b * NCH
                pe.wait_ge(out_ready, b * (NCH * KT))
                pe.wait_ge(stk_copied, gq0 + NCH)
                pe.wait_ge(v_lo, gq0 + NCH + 1)
                first_max_chunk(gq0, NCH - 1, gq0 + NCH)
                max_rows(gq0)
                for i in range(LEAD):
                    scores(gq0, 0, i)
                    for idx in range(MAX_EARLY * i // LEAD, MAX_EARLY * (i + 1) // LEAD):
                        max_tile(gq0 + 1, 1, idx)
                with pe.Fori(0, NCH - 2) as g:
                    group(b * NCH + g, g, 2)
                group(gq0 + (NCH - 2), NCH - 2, 1)
                group(gq0 + (NCH - 1), NCH - 1, 0)

            def first_a(j, pair, late):
                tokens(j + 1, 1, range(TPC), pair + 1)
                turn_stacks(j, 0, 2)
                first_max_chunk(0, j, j + 1)
                if late == 2:
                    tokens(j + 2, 0, range(TPC), pair + 2)
                turn_stacks(j + 1, 1, 2)
                if late == 2:
                    first_max_chunk(0, j + 1, j + 2)

            tokens(0, 0, range(TPC), 1)
            with pe.Fori(0, NA - 1) as jj:
                first_a(jj * 2, jj, 2)
            first_a(NCH - 2, NA - 1, 1)
            with pe.Fori(0, B - 1) as b:
                phase_b(b)
                phase_c(b, True)
            phase_b(B - 1)
            phase_c(B - 1, False)

        @block.scalar
        def _(act):
            act.sem_inc(exp_done, 2)
            act.sem_inc(g_ready, len(TILE_BANKS))

            def take_tokens(qa, s):
                act.wait_ge(skip_lo, qa)
                for t in range(TPC):
                    act.wait_ge(tok_ready, qa * TPC + t + 1)
                    act.activation(xt[:, s, t, :], ps[:, TILE_BANKS[t], :], ACT.Copy).then_inc(tok_taken, 1)

            def skip_values(qa, j, s):
                act.wait_ge(a_qkv, qa * 4 + 1)
                for t in range(TPC):
                    last = act.activation(xt[:, s, t, PD:C], xt[:, s, t, PD:C], ACT.Relu,
                                          bias=skip_b[:, s, t:t + 1], scale=skip_s[:, s, t:t + 1])
                last.then_inc(skip_f, 1)
                act.wait_ge(skip_f, qa + 1)
                act.activation(xm_hi[:, ds(j * TPC, TPC), PD:C], xt[:, s, :, PD:C], ACT.Copy).then_inc(skip_hi, 1)

            def copy_stacks(qa, j, bank):
                act.wait_ge(stk_turned, qa + 1)
                src = bank16(bank, BF16)
                act.activation(ks[0:NROW, ds(j * CH, CH)], src[0:NROW, 0:CH], ACT.Copy)
                act.activation(qs[0:NSTK, ds(j * CH, CH)], src[0:NSTK, CH:2 * CH], ACT.Copy).then_inc(stk_copied, 1)

            def exponentials(gq, i):
                n = gq * NU + i
                scores = ps[:, 2 * (i % 2):2 * (i % 2) + 2, :]
                act.wait_ge(st_ready, n + 1)
                if i in ACT_HIGH:
                    act.wait_ge(pv_done, n + 1)
                    act.activation(p_hi[:, i % RING, :].rearrange("p (h n) -> p h n", h=KPU), scores, ACT.Exp,
                                   scale=SCALE).then_inc(high_act, 1)
                j = (i - RING) % NU
                if j in POOL_LOW:
                    act.wait_ge(low_pool, (gq + (1 if i >= RING else 0)) * len(POOL_LOW) + (POOL_LOW.index(j) + 1))
                else:
                    act.wait_ge(low_dve, (gq + (1 if i >= RING else 0)) * len(DVE_LOW) + (DVE_LOW.index(j) + 1))
                act.activation(p32[:, i % RING, :].rearrange("p (h n) -> p h n", h=KPU), scores, ACT.Exp,
                               scale=SCALE).then_inc(exp_done, 1)

            def group(gq, last=False):
                for i in range(NU):
                    exponentials(gq, i)
                    if last and i in EARLY_OUT:
                        project_out(gq - (NCH - 1), EARLY_OUT.index(i))

            def project_out(q, o):
                act.wait_ge(y_ready, q * KT + o + 1)
                act.wait_ge(x1_ready, q * KT)
                act.activation(yb[:, o, :], ps[:, 4 + o % 2, :], ACT.Identity,
                               bias=shift2[:, o:o + 1], scale=wp_unscale[:, o:o + 1]).then_inc(y_scaled, 1)

            def gelu(q, j):
                act.wait_ge(h_ready, q * JT + j + 1)
                act.activation(gel[:, j, :], ps[:, TILE_BANKS[j % 4], :], ACT.Gelu,
                               scale=gelu_scale[:, j:j + 1]).then_inc(g_ready, 1)

            def chunk_c(b, j, s, late, with_next):
                q = b * NCH + j
                qa = q + NCH
                if with_next:
                    take_tokens(qa, s)
                act.wait_ge(z_ready, q)
                for n in range(JT):
                    gelu(q, n)
                    if late >= 1 and n in OUT_AT:
                        project_out(q + 1, OUT_AT.index(n))
                if with_next:
                    copy_stacks(qa, j, STK_BANK)
                    skip_values(qa, j, s)

            def phase_c(b, with_next):
                with act.Fori(0, NCH // 2 - 1) as jj:
                    act.activation(table[:, :], half[:, :], ACT.Gelu)
                    for s in range(2):
                        chunk_c(b, jj * 2 + s, s, 2, with_next)
                chunk_c(b, NCH - 2, 0, 1, with_next)
                chunk_c(b, NCH - 1, 1, 0, with_next)

            def phase_b(b):
                with act.Fori(0, NCH - 1) as g:
                    group(b * NCH + g)
                group(b * NCH + (NCH - 1), last=True)

            act.wait_ge(set_pe, 5)
            for k in range(KT):
                src = bank16((6, 7, 0)[k], F16)
                act.activation(wp_hi[:, k, :], src[:, 0:C], ACT.Copy)
                act.activation(wp_lo[:, k, :], src[:, 512:512 + C], ACT.Copy)
            act.activation(fc1[:, 0:1024], bank16(1, F16)[0:3 * DR, :], ACT.Copy)
            act.activation(fc1[:, 1024:DFF], bank16(2, F16)[0:3 * DR, 0:512], ACT.Copy).then_inc(set_up, 1)
            act.wait_ge(set_up, 2)

            def first_a(j, late):
                for s in range(2):
                    if s == 0 or late == 2:
                        take_tokens(j + (s + 1), 1 - s)
                    copy_stacks(j + s, j + s, 2)
                    skip_values(j + s, j + s, s)

            take_tokens(0, 0)
            with act.Fori(0, NA - 1) as jj:
                first_a(jj * 2, 2)
            first_a(NCH - 2, 1)
            with act.Fori(0, B - 1) as b:
                phase_b(b)
                phase_c(b, True)
            phase_b(B - 1)
            phase_c(B - 1, False)

        @block.vector
        def _(v):
            v.sem_inc(x_free[0], 1)
            v.sem_inc(x_free[1], 1)
            v.sem_inc(mx_free, 2)
            v.sem_inc(low_dve, len(DVE_LOW))
            v.sem_inc(pv_done, RING)
            steps = [0]

            def link(ins):
                steps[0] += 1
                ins.then_inc(set_dve, 1)
                v.wait_ge(set_dve, steps[0])

            link(v.memset(ones[:, :], 1.0))
            link(v.memset(expo[:, :], -0.5))
            link(v.memset(half[:, :], 0.5))
            link(v.memset(stk[:, :, :, :], 1.0))
            link(v.memset(vs[:, :, :], 1.0))
            v.wait_ge(w_loaded, 16 * N_LOADS)
            link(v.tensor_copy(ident_h[:, :], ident[:, :]))
            link(v.tensor_copy(ident_b[:, :], ident[:, :]))
            link(v.tensor_scalar(bvar[:, 0:1], bn1[:, 3:4], BN_EPS, None, ALU.add))
            link(v.tensor_scalar(bvar[:, 1:4], bn2[:, 3, :], BN_EPS, None, ALU.add))
            v.sem_inc(bn_var_ready, 1)
            v.wait_ge(set_pool, 1)
            link(v.tensor_tensor(binv[:, 0:1], binv[:, 0:1], bn1[:, 0:1], ALU.mult))
            link(v.tensor_tensor(binv[:, 1:4], binv[:, 1:4], bn2[:, 0, :], ALU.mult))
            link(v.tensor_tensor(junk, raw_qkv[:, :], lnb[:, :], ALU.mult))
            link(v.tensor_reduce(sc[:, 0:1], junk, AX.X, ALU.add))
            link(v.tensor_tensor(sc[:, 0:1], sc[:, 0:1], bn1[:, 2:3], ALU.subtract))
            link(v.scalar_tensor_tensor(sc[:, 0:1], sc[:, 0:1], binv[:, 0:1], bn1[:, 1:2], ALU.mult, ALU.add))
            link(v.scalar_tensor_tensor(w1, raw_qkv[:, :], binv[:, 0:1], lnw[:, :], ALU.mult, ALU.mult))
            link(v.tensor_reduce(sc[:, 1:2], w1, AX.X, ALU.add))
            link(v.tensor_scalar(sc[:, 1:2], sc[:, 1:2], 1.0 / PD, None, ALU.mult))
            link(v.tensor_scalar(w1, w1, sc[:, 1:2], None, ALU.subtract))
            link(v.tensor_tensor(junk, w1, w1, ALU.mult))
            link(v.tensor_reduce(sc[:, 2:3], junk, AX.X, ALU.add))
            link(v.tensor_scalar(sc[:, 2:3], sc[:, 2:3], float(PD), None, ALU.mult))
            v.sem_inc(norm_ready, 1)
            v.wait_ge(set_pool, 2)
            link(v.tensor_reduce(sc[:, 3:4], sc[:, 0:1], AX.X, ALU.max, apply_absolute_value=True))
            link(v.tensor_tensor(sc[:, 3:4], sc[:, 3:4], sc[:, 4:5], ALU.add))
            link(v.tensor_scalar(sc[:, 3:4], sc[:, 3:4], TINY, 1.0 / F16_TOP, ALU.max, ALU.mult))
            link(v.memset(sc[0:2 * QK, 3:4], 1.0))
            link(v.reciprocal(sc[:, 5:6], sc[:, 3:4]))
            link(v.tensor_scalar(w1, w1, sc[:, 5:6], None, ALU.mult))
            link(v.tensor_tensor(sc[:, 6:7], sc[:, 0:1], sc[:, 5:6], ALU.mult))
            link(v.tensor_scalar(diag[:, :], ident[:, :], sc[:, 6:7], None, ALU.mult))
            v.sem_inc(w1_ready, 1)
            v.wait_ge(set_pe, 1)
            link(v.tensor_copy(w_qkv[:, :], ps[0:PD, 0, 0:P]))
            link(v.tensor_copy(bias_qkv[:, :], ps[:, 1, 0:P]))
            link(v.tensor_scalar(p2b[:, :], ones[0:DB, :], fccol[:, 1:2], None, ALU.mult))
            link(v.tensor_reduce(fccol[:, 2:3], fccol[:, 0:1], AX.X, ALU.max, apply_absolute_value=True))
            link(v.tensor_scalar(diag[:, :], ident[:, :], sc[:, 3:4], None, ALU.mult))
            v.sem_inc(tau_ready, 1)
            v.wait_ge(set_pe, 2)
            link(v.tensor_copy(colscale[:, 0:PD], ps[:, 2, 0:PD]))
            link(v.memset(colscale[:, PD:C], 1.0 / SKIP_SCALE))
            for o in range(KT):
                link(v.scalar_tensor_tensor(raw_p[:, o, :], raw_p[:, o, :], binv[:, 1 + o:2 + o], colscale,
                                            ALU.mult, ALU.mult))
            link(v.tensor_reduce(wmax[:, :], raw_p, AX.X, ALU.max, apply_absolute_value=True))
            link(v.tensor_scalar(wp_unscale[:, :], wmax[:, :], TINY, 1.0 / W_TOP, ALU.max, ALU.mult))
            link(v.reciprocal(wmax[:, :], wp_unscale[:, :]))
            for o in range(KT):
                link(v.tensor_scalar(raw_p[:, o, :], raw_p[:, o, :], wmax[:, o:o + 1], None, ALU.mult))
            link(v.tensor_copy(wph0, raw_p))
            link(v.tensor_tensor(wpl0, raw_p, wph0, ALU.subtract))
            link(v.tensor_tensor(shift2[:, :], bn2[:, 2, :], binv[:, 1:4], ALU.mult))
            link(v.tensor_tensor(shift2[:, :], bn2[:, 1, :], shift2[:, :], ALU.subtract))
            link(v.tensor_reduce(fmax[:, :], raw_f, AX.X, ALU.max, apply_absolute_value=True))
            link(v.tensor_scalar(fmax[:, :], fmax[:, :], TINY, 1.0 / F16_TOP, ALU.max, ALU.mult))
            link(v.reciprocal(fsig[:, :], fmax[:, :]))
            link(v.tensor_tensor(raw_f, raw_f, fsig[:, :].unsqueeze(2).to_broadcast([P, JT, DR]), ALU.mult))
            link(v.tensor_copy(fstk[:, :, 0:DR], raw_f))
            link(v.tensor_copy(fstk[:, :, 2 * DR:3 * DR], raw_f))
            link(v.tensor_tensor(fstk[:, :, DR:2 * DR], raw_f, fstk[:, :, 0:DR], ALU.subtract))
            v.sem_inc(wp_ready, 1)
            v.wait_ge(set_pe, 3)
            link(v.tensor_scalar(sc[:, 7:8], ps[:, 3, 0:1], 1.0 / C, None, ALU.mult))
            link(v.tensor_scalar(sc[:, 8:9], ps[:, 3, 1:2], TINY, 1.0 / U_SCALE, ALU.max, ALU.mult))
            link(v.tensor_copy(sc[:, 10:13], ps[:, 3, 2:5]))
            link(v.reciprocal(sc[:, 9:10], sc[:, 8:9]))
            for k in range(KT):
                link(v.tensor_scalar(fold[:, k, :], blk[:, k, :], sc[:, 10 + k:11 + k], sc[:, 7:8],
                                     ALU.mult, ALU.subtract))
            link(v.tensor_scalar(fold[:, :, :], fold[:, :, :], sc[:, 9:10], None, ALU.mult))
            link(v.tensor_scalar(gelu_scale[:, :], fmax[:, :], sc[:, 8:9], None, ALU.mult))
            link(v.tensor_tensor(spread[:, :], ps[:, 4, 0:C], blkt[:, :], ALU.mult))
            v.wait_ge(set_pe, 4)
            link(v.tensor_copy(p1t[:, :, :], ps[:, 5, 0:JT * DR].rearrange("p (j a) -> p j a", j=JT)))
            v.sem_inc(set_up, 1)

            def statistics_of(q, s, tiles):
                for t in tiles:
                    v.wait_ge(tok_taken, q * TPC + t + 1)
                    v.bn_stats(bst[:, s, t, 0, :], xt[:, s, t, 0:C])
                    v.bn_stats(bst[:, s, t, 1, :], xt[:, s, t, 0:PD]).then_inc(a_stat, 1)

            def statistics(q, s, buf, done=0):
                statistics_of(q, s, range(done, TPC))
                v.sem_inc(x_free[buf], 1)
                v.wait_ge(a_stat, q * (TPC + 2) + TPC)
                v.sem_inc(passed, 1)
                for t in range(TPC):
                    v.bn_aggr(mv[:, s, t, 0, :], bst[:, s, t, 0, :])
                    last = v.bn_aggr(mv[:, s, t, 1, :], bst[:, s, t, 1, :])
                last.then_inc(a_stat, 1)
                v.wait_ge(a_stat, q * (TPC + 2) + TPC + 1)
                v.tensor_scalar(var[:, s, 0, :], mv[:, s, :, 0, 1], LN_IN_EPS, None, ALU.add).then_inc(a_stat, 1)
                v.wait_ge(a_stat, q * (TPC + 2) + TPC + 2)
                v.scalar_tensor_tensor(var[:, s, 1, :], var[:, s, 0, :], LN_ATTN_EPS, mv[:, s, :, 1, 1],
                                       ALU.mult, ALU.add).then_inc(a_var, 1)

            def qkv_parts(q, j, s):
                qkv_scaled(q, j, s)
                qkv_split(q, s)

            def qkv_scaled(q, j, s):
                v.wait_ge(a_rstd, q + 1)
                v.tensor_scalar(skip_s[:, s, :], rstd[:, s, 0, :], SKIP_SCALE, None, ALU.mult).then_inc(a_skip, 1)
                v.wait_ge(a_skip, q * 2 + 1)
                v.scalar_tensor_tensor(skip_b[:, s, :], mv[:, s, :, 0, 0], -1.0, skip_s[:, s, :],
                                       ALU.mult, ALU.mult).then_inc(a_skip, 1)
                v.wait_ge(v_lo, q)
                for t in range(TPC):
                    last = v.scalar_tensor_tensor(qkvf[:, s, t, :], xt[:, s, t, C:C + QKV], rstd[:, s, 1, t:t + 1],
                                                  bias_qkv[:, :], ALU.mult, ALU.add)
                last.then_inc(a_qkv, 1)
                v.wait_ge(a_qkv, q * 4 + 1)
                v.tensor_copy(parts[:, s, :, 0, :], qkvf[:, s, :, 0:2 * QK]).then_inc(a_qkv, 1)
                v.tensor_copy(vs[:, ds(j * TPC, TPC), 0:PD], qkvf[:, s, :, 2 * QK:]).then_inc(v_hi, 1)

            def qkv_split(q, s):
                v.wait_ge(a_qkv, q * 4 + 2)
                v.tensor_tensor(rest[:, s, :, :], qkvf[:, s, :, 0:2 * QK], parts[:, s, :, 0, :],
                                ALU.subtract).then_inc(a_qkv, 1)
                v.wait_ge(a_qkv, q * 4 + 3)
                v.tensor_copy(parts[:, s, :, 1, :], rest[:, s, :, :]).then_inc(a_qkv, 1)
                v.wait_ge(a_qkv, q * 4 + 4)
                v.tensor_tensor(parts[:, s, :, 2, :], rest[:, s, :, :], parts[:, s, :, 1, :],
                                ALU.subtract).then_inc(a_parts, 1)
                v.wait_ge(a_parts, q + 1)
                for lo, n in ((0, 3), (3, 2), (5, 1)):
                    v.tensor_copy(stk[:, s, :, lo * QK:(lo + n) * QK].rearrange("p t (l c) -> p t l c", l=n),
                                  parts[:, s, :, 0:n, QK:2 * QK])
                for part, (lo, n) in enumerate(((0, 3), (3, 2), (5, 1))):
                    last = v.tensor_copy(stk[:, s, :, P + lo * QK:P + (lo + n) * QK].rearrange("p t (l c) -> p t l c", l=n),
                                         parts[:, s, :, part:part + 1, 0:QK].to_broadcast([P, TPC, n, QK]))
                last.then_inc(stk_ready, 1)

            def max_tile(gq, idx):
                t, c = divmod(idx, NCH)
                v.wait_ge(mx_ready, gq * (NMX + 1) + idx + 1)
                v.tensor_reduce(mxp[:, t, c:c + 1], ps[:, 4 + idx % 2, :], AX.X, ALU.max).then_inc(mx_free, 1)

            def first_max_tile(base, c, t, bank):
                v.wait_ge(mx_ready, base + t + 1)
                v.tensor_reduce(mxp[:, t, ds(c, 1)], ps[:, bank, :], AX.X, ALU.max).then_inc(mx_free, 1)

            def first_max_chunk(gq, c):
                for t in range(TPC):
                    first_max_tile(gq * (NMX + 1) + c * TPC, c, t, 4 + t % 2)

            def max_parts(gq):
                v.wait_ge(mx_free, gq * MXC + NMX + 2)
                v.tensor_reduce(nmr[:, :], mxp[:, :, :], AX.X, ALU.max, negate=True).then_inc(nm_step, 1)
                v.wait_ge(nm_step, gq * 6 + 1)
                v.tensor_scalar(nm[:, :], nmr[:, :], EXP_SHIFT, None, ALU.add).then_inc(nm_step, 1)
                v.wait_ge(nm_step, gq * 6 + 2)
                v.tensor_copy(nms[:, :, 0], nm[:, :]).then_inc(nm_step, 1)
                v.wait_ge(nm_step, gq * 6 + 3)
                v.tensor_tensor(nmr[:, :], nm[:, :], nms[:, :, 0], ALU.subtract).then_inc(nm_step, 1)
                v.wait_ge(nm_step, gq * 6 + 4)
                v.tensor_copy(nms[:, :, 1], nmr[:, :]).then_inc(nm_step, 1)
                v.wait_ge(nm_step, gq * 6 + 5)
                v.tensor_tensor(nms[:, :, 2], nmr[:, :], nms[:, :, 1], ALU.subtract).then_inc(nm_step, 1)

            def max_rows(gq, g):
                v.wait_ge(mx_ready, (gq + 1) * (NMX + 1))
                v.tensor_copy(qs[NSTK:NROW, ds(g * CH, CH)], bank16(4, BF16)[0:3, 0:CH]).then_inc(mx_free, 2)

            def high_low(gq, i):
                n = gq * NU + i
                if i in DVE_HIGH:
                    v.wait_ge(exp_done, n + 3)
                    v.wait_ge(pv_done, n + 1)
                    v.tensor_copy(p_hi[:, i % RING, :], p32[:, i % RING, :]).then_inc(high_dve, 1)
                if i in DVE_LOW:
                    if i in DVE_HIGH:
                        v.wait_ge(high_dve, gq * len(DVE_HIGH) + (DVE_HIGH.index(i) + 1))
                    else:
                        v.wait_ge(high_act, gq * len(ACT_HIGH) + (ACT_HIGH.index(i) + 1))
                        v.wait_ge(exp_done, n + 3)
                    v.tensor_tensor(p_lo[:, i % RING, :], p32[:, i % RING, :], p_hi[:, i % RING, :],
                                    ALU.subtract).then_inc(low_dve, 1)

            def take_accumulators(gq):
                v.wait_ge(pv_done, (gq + 1) * NU + RING)
                for h in range(2):
                    v.tensor_copy(acs[:, 2 * h:2 * h + 2, 0:VN],
                                  ps[:, 6 + h, 0:2 * VP].rearrange("p (t n) -> p t n", t=2)[:, :, 0:VN]
                                  ).then_inc(acs_ready, 1)

            def finish_group(gq, g, step):
                at = ds(g * TPC, TPC)
                if step == 0:
                    v.wait_ge(acs_ready, (gq + 1) * 2)
                    v.reciprocal(rsum[:, :], acs[:, :, PD]).then_inc(post, 1)
                    v.tensor_tensor(attn[:, :, :], acs[:, :, 0:PD], acs[:, :, PD + 1:VN], ALU.add).then_inc(post, 1)
                if step == 1:
                    v.wait_ge(post, gq * 5 + 2)
                    v.scalar_tensor_tensor(attn[:, :, :], attn[:, :, :], 0.0,
                                           rsum[:, :].unsqueeze(2).to_broadcast([P, TPC, PD]),
                                           ALU.max, ALU.mult).then_inc(post, 1)
                if step == 2:
                    v.wait_ge(post, gq * 5 + 3)
                    v.tensor_copy(xm_hi[:, at, 0:PD], attn[:, :, :]).then_inc(post, 1)
                if step == 3:
                    v.wait_ge(post, gq * 5 + 4)
                    v.tensor_tensor(xm_lo[:, at, 0:PD], attn[:, :, :], xm_hi[:, at, 0:PD], ALU.subtract).then_inc(post, 1)

            def group(gq, g, first, left, b=None):
                q0 = gq - (NCH - 1)
                for i in range(NU):
                    if i == 0 and not first:
                        take_accumulators(gq - 1)
                    for idx in max_tiles_at(i):
                        if i < MAX_ROWS_AT and left >= 1:
                            max_tile(gq + 1, idx)
                        if i > MAX_ROWS_AT and left >= 2:
                            max_tile(gq + 2, idx)
                    if i == MAX_ROWS_AT - 1 and left >= 1:
                        max_parts(gq + 1)
                    if i + 1 < NU:
                        high_low(gq, i + 1)
                    elif left >= 1:
                        high_low(gq + 1, 0)
                    if i == MAX_ROWS_AT and left >= 1:
                        max_rows(gq + 1, g + 1)
                    if i in FINISH_AT and not first:
                        finish_group(gq - 1, g - 1, FINISH_AT.index(i))
                    if left == 0 and i in EARLY_COPIES:
                        j, k, bank = EARLY_COPIES[i]
                        copy_turned(q0 + j, k, bank)
                    if left == 0 and i in EARLY_OUT:
                        residual(q0, 0, EARLY_OUT.index(i), b * (NCH // 2))

            def copy_turned(q, k, bank):
                v.wait_ge(xt_ready, q * KT + k + 1)
                v.tensor_copy(xc[:, k, :, :].rearrange("p a n -> p (a n)"),
                              bank16(bank, F16)).then_inc(xt_copied, 1)

            def residual(q, s, o, stores):
                if o == 0:
                    v.wait_ge(stored[s], stores * 16)
                    v.wait_ge(x_loaded[0], (q + (NA + 1)) * 16)
                v.wait_ge(y_scaled, q * KT + o + 1)
                v.tensor_tensor(x1[:, s, o, :], yb[:, o, :], xin[:, 0, o, :], ALU.add).then_inc(x1_ready, 1)
                if o == KT - 1:
                    v.wait_ge(x1_ready, (q + 1) * KT)
                    v.sem_inc(x_free[0], 1)

            def folded(q, s):
                v.wait_ge(u_ready, q + 1)
                v.tensor_copy(uraw[:, :], ps[:, 3, 0:P]).then_inc(u_taken, 1)
                for t in range(TPC):
                    v.wait_ge(x1t_ready, q * TPC + t + 1)
                    v.bn_stats(cst[:, s, t, :], ps[:, TILE_BANKS[t], 0:C]).then_inc(c_stat, 1)
                v.wait_ge(c_stat, q * (TPC + 1) + TPC)
                v.sem_inc(passed, 1)
                for t in range(TPC):
                    last = v.bn_aggr(cmv[:, s, t, :], cst[:, s, t, :])
                last.then_inc(c_stat, 1)
                v.wait_ge(c_stat, q * (TPC + 1) + TPC + 1)
                v.tensor_scalar(cvar[:, s, :], cmv[:, s, :, 1], LN_FFN_EPS, None, ALU.add).then_inc(c_var, 1)

            def split_u(q, s):
                v.wait_ge(c_rstd, q + 1)
                v.wait_ge(u_turned, q + 1)
                v.tensor_tensor(uf[:, s, :, :], ps[:, 3, 0:P].rearrange("p (t a) -> p t a", t=TPC),
                                crstd[:, s, :].unsqueeze(2).to_broadcast([P, TPC, DR]), ALU.mult).then_inc(u_split, 1)
                v.wait_ge(u_split, q * 4 + 1)
                v.tensor_copy(us[:, s, :, 0:DR], uf[:, s, :, :]).then_inc(u_split, 1)
                v.tensor_copy(us[:, s, :, DR:2 * DR], uf[:, s, :, :]).then_inc(u_split, 1)
                v.wait_ge(u_split, q * 4 + 2)
                v.tensor_tensor(us[:, s, :, 2 * DR:3 * DR], uf[:, s, :, :], us[:, s, :, 0:DR],
                                ALU.subtract).then_inc(u_split, 1)

            def copy_u(q):
                v.wait_ge(ut_ready, q + 1)
                v.tensor_copy(uc[:, :], bank16(3, F16)[0:3 * DR, 0:CH]).then_inc(ut_copied, 1)

            def copy_z(q):
                v.wait_ge(z_ready, q + 1)
                v.tensor_copy(zs[:, :], ps[:, 3, :]).then_inc(z_copied, 1)

            def results(q, s, tiles):
                for o in tiles:
                    v.wait_ge(ff_ready, q * KT + o + 1)
                    v.tensor_tensor(x1[:, s, o, :], ps[:, EXPAND_BANKS[o], :], x1[:, s, o, :], ALU.add).then_inc(out_ready, 1)

            def chunk_c(b, j, s, pair, late, with_next, next_max=True):
                def max_for_next(*tiles):
                    for t in tiles:
                        if with_next and next_max:
                            first_max_tile((b + 1) * NCH * (NMX + 1) + (j - 1) * TPC, j - 1, t, FIRST_MAX_BANK)

                q = b * NCH + j
                qa = q + NCH
                if with_next:
                    statistics_of(qa, s, range(1))
                copy_u(q)
                if with_next:
                    statistics(qa, s, 1, done=1)
                max_for_next(0)
                if late >= 1:
                    residual(q + 1, 1 - s, 0, b * (NCH // 2) + pair + s)
                max_for_next(1)
                if with_next:
                    qkv_scaled(qa, j, s)
                max_for_next(2)
                if with_next:
                    qkv_split(qa, s)
                if late >= 1:
                    residual(q + 1, 1 - s, 1, 0)
                max_for_next(3)
                if late >= 1:
                    residual(q + 1, 1 - s, 2, 0)
                if late >= 2:
                    copy_turned(q + 2, 0, XT_BANKS[0])
                copy_z(q)
                if late >= 2:
                    copy_turned(q + 2, 1, XT_BANKS[1])
                    copy_turned(q + 2, 2, XT_BANKS[2])
                if late >= 1:
                    folded(q + 1, 1 - s)
                results(q, s, range(1))
                if late >= 1:
                    split_u(q + 1, 1 - s)
                results(q, s, range(1, KT))

            def phase_c(b, with_next):
                q0 = b * NCH
                copy_turned(q0 + 1, 2, EARLY_TURNS[NU - 1][2])
                take_accumulators(q0 + (NCH - 1))
                folded(q0, 0)
                for step in range(2):
                    finish_group(q0 + (NCH - 1), NCH - 1, step)
                split_u(q0, 0)
                for step in range(2, len(FINISH_AT)):
                    finish_group(q0 + (NCH - 1), NCH - 1, step)
                for s in range(2):
                    chunk_c(b, s, s, 0, 2, with_next, next_max=s > 0)
                with v.Fori(1, NCH // 2 - 1) as jj:
                    for s in range(2):
                        chunk_c(b, jj * 2 + s, s, jj, 2, with_next)
                chunk_c(b, NCH - 2, 0, NCH // 2 - 1, 1, with_next)
                chunk_c(b, NCH - 1, 1, NCH // 2 - 1, 0, with_next)

            def phase_b(b):
                gq0 = b * NCH
                first_max_chunk(gq0, NCH - 1)
                max_parts(gq0)
                max_rows(gq0, 0)
                for idx in range(MAX_EARLY):
                    max_tile(gq0 + 1, idx)
                high_low(gq0, 0)
                group(gq0, 0, True, 2)
                with v.Fori(1, NCH - 2) as g:
                    group(b * NCH + g, g, False, 2)
                group(gq0 + (NCH - 2), NCH - 2, False, 1)
                group(gq0 + (NCH - 1), NCH - 1, False, 0, b)

            def first_a(j, late):
                for s in range(2):
                    qkv_parts(j + s, j + s, s)
                    if s == 0 or late == 2:
                        statistics(j + (s + 1), 1 - s, 1 - s)
                        first_max_chunk(0, j + s)

            statistics(0, 0, 0)
            with v.Fori(0, NA - 1) as jj:
                first_a(jj * 2, 2)
            first_a(NCH - 2, 1)
            with v.Fori(0, B - 1) as b:
                phase_b(b)
                phase_c(b, True)
            phase_b(B - 1)
            phase_c(B - 1, False)

        @block.gpsimd
        def _(g):
            g.sem_inc(low_pool, len(POOL_LOW))
            g.sem_inc(skip_lo, 1)
            g.sem_inc(v_lo, 1)
            g.wait_ge(bn_var_ready, 1)
            g.tensor_tensor(binv[:, :], bvar[:, :], expo[:, 0:4], ALU.pow).then_inc(set_pool, 1)
            g.wait_ge(norm_ready, 1)
            g.tensor_tensor(sc[:, 4:5], sc[:, 2:3], half[:, :], ALU.pow).then_inc(set_pool, 1)

            def rstd_a(q, s):
                g.wait_ge(a_var, q + 1)
                g.tensor_tensor(rstd[:, s, :, :].rearrange("p a t -> p (a t)"),
                                var[:, s, :, :].rearrange("p a t -> p (a t)"), expo[:, :], ALU.pow).then_inc(a_rstd, 1)

            def low_v(q, j, s):
                tiles = ds(j * TPC, TPC)
                g.wait_ge(v_hi, q + 1)
                g.tensor_tensor(vs[:, tiles, PD + 1:VN], qkvf[:, s, :, 2 * QK:], vs[:, tiles, 0:PD],
                                ALU.subtract).then_inc(v_lo, 1)

            def low_skip(q, j, s):
                tiles = ds(j * TPC, TPC)
                g.wait_ge(skip_hi, q + 1)
                g.tensor_tensor(xm_lo[:, tiles, PD:C], xt[:, s, :, PD:C], xm_hi[:, tiles, PD:C],
                                ALU.subtract).then_inc(skip_lo, 1)

            def low_parts(gq):
                for i in POOL_LOW:
                    if i in DVE_HIGH:
                        g.wait_ge(high_dve, gq * len(DVE_HIGH) + (DVE_HIGH.index(i) + 1))
                    else:
                        g.wait_ge(high_act, gq * len(ACT_HIGH) + (ACT_HIGH.index(i) + 1))
                    g.wait_ge(exp_done, gq * NU + i + 3)
                    g.tensor_tensor(p_lo[:, i % RING, :], p32[:, i % RING, :], p_hi[:, i % RING, :],
                                    ALU.subtract).then_inc(low_pool, 1)

            def rstd_c(q, s):
                g.wait_ge(c_var, q + 1)
                g.tensor_tensor(crstd[:, s, :], cvar[:, s, :], expo[:, 0:TPC], ALU.pow).then_inc(c_rstd, 1)

            def chunk_c(b, j, s, late, with_next):
                q = b * NCH + j
                if with_next:
                    rstd_a(q + NCH, s)
                    low_v(q + NCH, j, s)
                if late >= 1:
                    rstd_c(q + 1, 1 - s)
                if with_next:
                    low_skip(q + NCH, j, s)

            def phases_bc(b, with_next):
                with g.Fori(0, NCH) as gr:
                    low_parts(b * NCH + gr)
                rstd_c(b * NCH, 0)
                with g.Fori(0, NCH // 2 - 1) as jj:
                    for s in range(2):
                        chunk_c(b, jj * 2 + s, s, 2, with_next)
                chunk_c(b, NCH - 2, 0, 1, with_next)
                chunk_c(b, NCH - 1, 1, 0, with_next)

            def first_a(j, late):
                for s in range(2):
                    if s == 0 or late == 2:
                        rstd_a(j + (s + 1), 1 - s)
                    low_v(j + s, j + s, s)
                    low_skip(j + s, j + s, s)

            rstd_a(0, 0)
            with g.Fori(0, NA - 1) as jj:
                first_a(jj * 2, 2)
            first_a(NCH - 2, 1)
            with g.Fori(0, B - 1) as b:
                phases_bc(b, True)
            phases_bc(B - 1, False)


_INS = {"x": "x", "L0_conv_ln_w": "ln_w", "L0_conv_ln_b": "ln_b", "L0_conv_w_qkv": "w_qkv",
        "L0_conv_bn1_g": "bn1_g", "L0_conv_bn1_b": "bn1_b", "L0_conv_bn1_m": "bn1_m", "L0_conv_bn1_v": "bn1_v",
        "L0_conv_w_proj": "w_proj", "L0_conv_bn2_g": "bn2_g", "L0_conv_bn2_b": "bn2_b", "L0_conv_bn2_m": "bn2_m",
        "L0_conv_bn2_v": "bn2_v", "L0_ffn_c_fc_1": "c_fc_1", "L0_ffn_c_fc_2": "c_fc_2",
        "L0_ffn_c_proj_1": "c_proj_1", "L0_ffn_c_proj_2": "c_proj_2"}


def shape_constants():
    ch = np.arange(C)
    blk = (ch[:, None] // DB == np.arange(DR)[None, :]).astype(np.float32)
    return {
        "ident": np.eye(P, dtype=np.float32),
        "rep": (ch[None, :] % DB == np.arange(DB)[:, None]).astype(np.float32),
        "blk": blk,
        "blkt": np.ascontiguousarray(np.concatenate([blk.T] * 4, axis=0)),
    }


def kernel(**inputs):
    import concourse.bacc as bacc
    from concourse.bass_utils import run_bass_kernel_spmd

    nc = bacc.Bacc("TRN2", target_bir_lowering=False, num_devices=1)
    arrays, aps = {}, {}
    for name, short in _INS.items():
        arrays[f"in_{short}"] = np.ascontiguousarray(inputs[name])
    for short, a in shape_constants().items():
        arrays[f"in_{short}"] = a
    for key, a in arrays.items():
        aps[key[3:]] = nc.dram_tensor(key, a.shape, mybir.dt.from_np(a.dtype), kind="ExternalInput").ap()
    aps["out"] = nc.dram_tensor("out_0", (B, C, H, W), F32, kind="ExternalOutput").ap()
    build(nc, aps)
    r = run_bass_kernel_spmd(nc, [arrays], core_ids=[0])
    return r.results[0]["out_0"]
```
